# Optimizing a Trainium2 kernel written in Bass

```python
import numpy as np
import jax
import jax.numpy as jnp

def _softmax(x, axis=-1):
    return jax.nn.softmax(x, axis=axis)

def _gelu(x):
    return jax.nn.gelu(x, approximate=True)

def _silu(x):
    return jax.nn.silu(x)

def _sigmoid(x):
    return jax.nn.sigmoid(x)

def _layernorm(x, axis=-1, eps=1e-05):
    m = jnp.mean(x, axis=axis, keepdims=True)
    v = jnp.var(x, axis=axis, keepdims=True)
    return (x - m) / jnp.sqrt(v + eps)

def _scatter_add(tgt, idx, src, axis=0):
    return tgt.at[idx].add(src)

def _segment_sum(src, seg, n):
    return jax.ops.segment_sum(src, seg, n)
kernel_name = 'mk_xattn_ffn_d1_seqx_r8_aa3909'

def setup_inputs(seed: int=0):
    np.random.seed(seed)
    _w = jnp.asarray

    def _rec_inputs():
        import jax
        import jax.numpy as jnp
        _rk = jax.random.key(seed)
        x = -0.0002928 + 1 * jax.random.normal(jax.random.fold_in(_rk, 1), (128, 64, 128), jnp.float32)
        _lenS = 64 - jax.random.randint(jax.random.fold_in(_rk, 7), (128,), 0, max(1, 64 // 4) + 1, jnp.int32)
        _lenS2 = 64 - jax.random.randint(jax.random.fold_in(_rk, 8), (128,), 0, max(1, 64 // 4) + 1, jnp.int32)
        _ctx_1024P = jax.random.normal(jax.random.fold_in(_rk, 11), (128, 16, 128), jnp.float32)
        _ctx_1024c = jax.random.dirichlet(jax.random.fold_in(_rk, 511), 0.3 * jnp.ones((16,), jnp.float32), (128, 64))
        _ctx_1024t = jnp.einsum('bsk,bkd->bsd', _ctx_1024c, _ctx_1024P)
        _ctx_1024t = _ctx_1024t * jax.lax.rsqrt(jnp.mean(jnp.square(_ctx_1024t)) + 1e-12) * 0.953939
        ctx_1024 = -1.39393e-06 + 0.999914 * (_ctx_1024t + 0.3 * jax.random.normal(jax.random.fold_in(_rk, 611), (128, 64, 128), jnp.float32))
        _validS = jnp.arange(64)[None, :] < _lenS[:, None]
        _validS2 = jnp.arange(64)[None, :] < _lenS2[:, None]
        _causal = jnp.tril(jnp.ones((64, 64), dtype=bool))
        mask_BxS2_bf0 = jnp.logical_not(jnp.ones((128, 64), dtype=bool))
        return (x, ctx_1024, mask_BxS2_bf0)
    x, ctx_1024, mask_BxS2_bf0 = _rec_inputs()

    def _L0_xattn_setup():
        import jax, jax.numpy as jnp
        import numpy as np
        DIM = 128
        HEADS = 16
        DIM_HEAD = 64
        INNER = HEADS * DIM_HEAD
        B, N = (2, 256)
        SCALE = DIM_HEAD ** (-0.5)
        key = jax.random.key(seed)
        ks = jax.random.split(key, 9)
        s_in = 1.0 / np.sqrt(DIM)
        s_inner = 1.0 / np.sqrt(INNER)
        return {'q': jax.random.normal(ks[0], (B, N, DIM), jnp.float32), 'k': jax.random.normal(ks[1], (B, N, DIM), jnp.float32), 'v': jax.random.normal(ks[2], (B, N, DIM), jnp.float32), 'Wq': jax.random.normal(ks[3], (DIM, INNER), jnp.float32) * s_in, 'Wk': jax.random.normal(ks[4], (DIM, INNER), jnp.float32) * s_in, 'Wv': jax.random.normal(ks[5], (DIM, INNER), jnp.float32) * s_in, 'Wo': jax.random.normal(ks[6], (INNER, DIM), jnp.float32) * s_inner, 'bo': jax.random.normal(ks[7], (DIM,), jnp.float32) * s_inner, 'mask': jnp.zeros((B, N), dtype=bool)}
    _L0_xattn_all = _L0_xattn_setup()
    _L0_xattn_in = {k: v for k, v in _L0_xattn_all.items() if k in ('Wq', 'Wk', 'Wv', 'Wo', 'bo')}
    del _L0_xattn_all

    def _L0_ffn_setup():
        import jax, jax.numpy as jnp
        import numpy as np
        E = 8
        TOP_K = 2
        LN_EPS = 1e-05

        def _layernorm(x, g, b):
            mu = jnp.mean(x, axis=-1, keepdims=True)
            var = jnp.var(x, axis=-1, keepdims=True)
            return (x - mu) * jax.lax.rsqrt(var + LN_EPS) * g + b
        key = jax.random.key(seed)
        ks = jax.random.split(key, 4)
        B, T, H, HF = (4, 256, 128, 256)
        s_in = 1.0 / np.sqrt(H)
        s_hid = 1.0 / np.sqrt(HF)
        return {'x': jax.random.normal(ks[0], (B, T, H), dtype=jnp.float32), 'ln_g': jnp.ones((H,), dtype=jnp.float32), 'ln_b': jnp.zeros((H,), dtype=jnp.float32), 'rW': jax.random.normal(ks[1], (H, E), dtype=jnp.float32) * s_in, 'rb': jnp.zeros((E,), dtype=jnp.float32), 'W1': jax.random.normal(ks[2], (E, H, HF), dtype=jnp.float32) * s_in, 'b1': jnp.zeros((E, HF), dtype=jnp.float32), 'W2': jax.random.normal(ks[3], (E, HF, H), dtype=jnp.float32) * s_hid, 'b2': jnp.zeros((E, H), dtype=jnp.float32)}
    _L0_ffn_all = _L0_ffn_setup()
    _L0_ffn_in = {k: v for k, v in _L0_ffn_all.items() if k in ('ln_g', 'ln_b', 'rW', 'rb', 'W1', 'b1', 'W2', 'b2')}
    del _L0_ffn_all
    return {'x': x, 'ctx_1024': ctx_1024, 'mask_BxS2_bf0': mask_BxS2_bf0, 'L0_xattn_Wq': _L0_xattn_in['Wq'], 'L0_xattn_Wk': _L0_xattn_in['Wk'], 'L0_xattn_Wv': _L0_xattn_in['Wv'], 'L0_xattn_Wo': _L0_xattn_in['Wo'], 'L0_xattn_bo': _L0_xattn_in['bo'], 'L0_ffn_ln_g': _L0_ffn_in['ln_g'], 'L0_ffn_ln_b': _L0_ffn_in['ln_b'], 'L0_ffn_rW': _L0_ffn_in['rW'], 'L0_ffn_rb': _L0_ffn_in['rb'], 'L0_ffn_W1': _L0_ffn_in['W1'], 'L0_ffn_b1': _L0_ffn_in['b1'], 'L0_ffn_W2': _L0_ffn_in['W2'], 'L0_ffn_b2': _L0_ffn_in['b2']}

def reference(x, ctx_1024, mask_BxS2_bf0, L0_xattn_Wq, L0_xattn_Wk, L0_xattn_Wv, L0_xattn_Wo, L0_xattn_bo, L0_ffn_ln_g, L0_ffn_ln_b, L0_ffn_rW, L0_ffn_rb, L0_ffn_W1, L0_ffn_b1, L0_ffn_W2, L0_ffn_b2):
    import jax
    import jax.numpy as jnp

    def _L0_xattn_ref(q, k, v, Wq, Wk, Wv, Wo, bo, mask):
        import jax, jax.numpy as jnp
        import numpy as np
        DIM = 128
        HEADS = 16
        DIM_HEAD = 64
        INNER = HEADS * DIM_HEAD
        B, N = (2, 256)
        SCALE = DIM_HEAD ** (-0.5)
        b, n, _ = q.shape
        h, d = (HEADS, DIM_HEAD)

        def split_heads(x):
            return x.reshape(b, n, h, d).transpose(0, 2, 1, 3)
        qh = split_heads(q @ Wq)
        kh = split_heads(k @ Wk)
        vh = split_heads(v @ Wv)
        dots = jnp.einsum('bhid,bhjd->bhij', qh, kh) * SCALE
        mask_value = -jnp.finfo(dots.dtype).max
        dots = jnp.where(mask[:, None, None, :], mask_value, dots)
        causal = jnp.triu(jnp.ones((n, n), dtype=bool), k=1)
        dots = jnp.where(causal[None, None, :, :], mask_value, dots)
        attn = jax.nn.softmax(dots, axis=-1)
        out = jnp.einsum('bhij,bhjd->bhid', attn, vh)
        out = out.transpose(0, 2, 1, 3).reshape(b, n, h * d)
        return out @ Wo + bo

    def _L0_ffn_ref(x, ln_g, ln_b, rW, rb, W1, b1, W2, b2):
        import jax, jax.numpy as jnp
        import numpy as np
        E = 8
        TOP_K = 2
        LN_EPS = 1e-05

        def _layernorm(x, g, b):
            mu = jnp.mean(x, axis=-1, keepdims=True)
            var = jnp.var(x, axis=-1, keepdims=True)
            return (x - mu) * jax.lax.rsqrt(var + LN_EPS) * g + b
        z = _layernorm(x, ln_g, ln_b)
        logits = jnp.einsum('bth,he->bte', z, rW) + rb
        probs = jax.nn.softmax(logits, axis=-1)
        topv, topi = jax.lax.top_k(probs, TOP_K)
        mask = jnp.sum(jax.nn.one_hot(topi, E, dtype=probs.dtype) * topv[..., None], axis=-2)
        denom = jnp.maximum(jnp.sum(mask, axis=-1, keepdims=True), 1e-08)
        w = mask / denom
        hid = jax.nn.gelu(jnp.einsum('bth,ehf->btef', z, W1) + b1, approximate=False)
        outs = jnp.einsum('btef,efh->bteh', hid, W2) + b2
        mixed = jnp.sum(outs * w[..., None], axis=2)
        return x + mixed
    x = x + _L0_xattn_ref(_layernorm(x, axis=-1), ctx_1024, ctx_1024, L0_xattn_Wq, L0_xattn_Wk, L0_xattn_Wv, L0_xattn_Wo, L0_xattn_bo, mask_BxS2_bf0)
    x = x + _L0_ffn_ref(_layernorm(x, axis=-1), L0_ffn_ln_g, L0_ffn_ln_b, L0_ffn_rW, L0_ffn_rb, L0_ffn_W1, L0_ffn_b1, L0_ffn_W2, L0_ffn_b2)
    return x

_drawn_inputs = setup_inputs


def setup_inputs(seed=0):
    import zlib

    import numpy as np

    out = dict(_drawn_inputs(seed))
    spreads = {'L0_ffn_ln_g': (1.0, 0.2),
     'L0_ffn_ln_b': (0.0, 0.1),
     'L0_ffn_rb': (0.0, 0.1),
     'L0_ffn_b1': (0.0, 0.354),
     'L0_ffn_b2': (0.0, 0.1)}
    factors = {}
    for name, (base, spread) in spreads.items():
        noise = np.random.default_rng([zlib.crc32(name.encode()), seed]).standard_normal(out[name].shape)
        drawn = base * np.exp(spread * noise) if base else spread * noise
        out[name] = jnp.asarray(drawn.astype(out[name].dtype))
    for name, factor in factors.items():
        out[name] = (out[name] * factor).astype(out[name].dtype)
    return out
```

```python
from contextlib import ExitStack

import concourse.bass as bass
from concourse import mybir

F32 = mybir.dt.float32
F32R = mybir.dt.float32r
BF16 = mybir.dt.bfloat16
U8 = mybir.dt.uint8
ALU = mybir.AluOpType
ACT = mybir.ActivationFunctionType
AX_X = mybir.AxisListType.X

P = 128
LN_EPS = 1e-5
NEG = -3.3895313892515355e38
EULER = 2.718281828459045

KEY_UNITS, VALUE_UNITS = 16, 16
UNITS = KEY_UNITS + VALUE_UNITS + 4
RING = 4


def unit_owner(idx):
    if idx < KEY_UNITS:
        return (1, 0) if idx % 2 == 0 else (0, 1)
    if idx < KEY_UNITS + VALUE_UNITS:
        return (2, 0)
    if idx < KEY_UNITS + VALUE_UNITS + 2:
        return (1, 0)
    return (1, 1)


ACT_PER_GROUP = sum(unit_owner(i)[0] for i in range(UNITS))
DVE_PER_GROUP = sum(unit_owner(i)[1] for i in range(UNITS))
PREP_ACT = sum(unit_owner(i)[0] for i in range(UNITS - 4, UNITS))
PREP_DVE = sum(unit_owner(i)[1] for i in range(UNITS - 4, UNITS))


def units_done(g, idx):
    return 4 + UNITS * g + idx + 1


def act_done(g, idx):
    if idx < 0:
        return PREP_ACT + ACT_PER_GROUP * g - sum(unit_owner(i)[0] for i in range(UNITS + idx + 1, UNITS))
    return PREP_ACT + ACT_PER_GROUP * g + sum(unit_owner(i)[0] for i in range(idx + 1))


def dve_done(g, idx):
    if idx < 0:
        return PREP_DVE + DVE_PER_GROUP * g - sum(unit_owner(i)[1] for i in range(UNITS + idx + 1, UNITS))
    return PREP_DVE + DVE_PER_GROUP * g + sum(unit_owner(i)[1] for i in range(idx + 1))


def xattn_ffn_kernel(nc, x, ctx_in, mask, Wq, Wk, Wv, Wo, bo, ln_g, ln_b, rW, rb, W1, b1, W2, b2, out):
    B, S, D = x.shape
    INNER = Wq.shape[1]
    DH = 64
    H = INNER // DH
    E, _, HF = W1.shape
    FC = HF // P
    NP = B * S // P
    GP = 4
    NG = NP // GP
    TG = GP * P
    assert S == 64 and D == P and H == 16 and E == 8 and FC == 2 and NG == 16

    x_t = x.rearrange("(n two) s d -> (two s) n d", two=2)
    c_t = ctx_in.rearrange("(n two) s d -> (two s) n d", two=2)
    out_t = out.rearrange("(n two) s d -> (two s) n d", two=2)

    with ExitStack() as es:
        def sb(name, shape, dt=F32):
            return es.enter_context(nc.sbuf_tensor(name, shape, dt))

        def sem(name):
            return es.enter_context(nc.semaphore(name))

        xs = sb("xs", [P, NP, D])
        c_in = sb("c_in", [P, GP, D])
        z = sb("z", [P, GP, D])
        zT = sb("zT", [P, TG])
        cTh = sb("cTh", [P, TG], F32R)
        cTl = sb("cTl", [P, TG], F32R)
        Ah = sb("Ah", [P, H, D], F32R)
        Al = sb("Al", [P, H, D], F32R)
        Nh = sb("Nh", [P, 2, H // 2, D], F32R)
        Nl = sb("Nl", [P, 2, H // 2, D], F32R)
        kf = sb("kf", [P, H, TG])
        vf = [sb(f"vf{i}", [P, 2, H // 2, D]) for i in range(2)]
        pr = [sb(f"pr{i}", [P, H, S]) for i in range(2)]
        pT = sb("pT", [P, H // 2, P])
        mask_b = sb("mask_b", [P, NP, S], BF16)
        W1h = sb("W1h", [P, E, HF], F32R)
        W1l = sb("W1l", [P, E, HF], F32R)
        W2s = sb("W2s", [P, E, FC, D])
        w1_raw = sb("w1_raw", [P, E, HF])
        ident = sb("ident", [P, P])
        ident_b = sb("ident_b", [P, P], BF16)
        causal = sb("causal", [P, P])
        causal_q = sb("causal_q", [P, S])
        sel2 = sb("sel2", [2, P], BF16)
        bo_b = sb("bo_b", [P, D])
        rb_b = sb("rb_b", [P, E])
        rW_s = sb("rW_s", [P, E])
        b2_s = sb("b2_s", [E, D])
        vec_rows = sb("vec_rows", [E * FC + 2, P])
        vec_cols = sb("vec_cols", [P, E * FC + 2])
        b1c = vec_cols[:, 0:E * FC]
        gc = vec_cols[:, E * FC:E * FC + 1]
        bc = vec_cols[:, E * FC + 1:E * FC + 2]
        rank = sb("rank", [P, E])
        half = sb("half", [P, GP])
        euler = sb("euler", [P, GP, E])
        mx = sb("mx", [P, 2, H])
        sm = sb("sm", [P, 2, H])
        ri = sb("ri", [P, 2, H])
        st = sb("st", [P, GP, 6])
        mv = sb("mv", [P, GP, 2])
        ve = sb("ve", [P, GP])
        rs = sb("rs", [P, GP])
        idle = sb("idle", [P, 1])

        wq_s = kf[:, 0:2, :]
        wk_s = kf[:, 2:4, :]
        wv_s = kf[:, 4:6, :]
        wo_s = kf[:, 6:8, :].rearrange("p a (j n) -> p (a j) n", n=D)
        wT = kf[:, 8:14, :].rearrange("p (w a) (j n) -> p w (a j) n", w=3, n=P)
        mask_raw = es.enter_context(nc.sbuf_tensor("mask_raw", [2, NP, S], U8))
        mask_row = vf[0][0:2, :, :, :].rearrange("p a j n -> p (a j n)").bitcast(BF16).rearrange(
            "p (n s) -> p n s", s=S)

        hid = [kf[:, i, :] for i in range(4)]
        xp = kf[:, 4, :].rearrange("p (t d) -> p t d", d=D)
        zn = kf[:, 5, :].rearrange("p (t d) -> p t d", d=D)
        z2T = [kf[:, 6 + i, :] for i in range(2)]
        z2h = [sb(f"z2h{i}", [P, TG], F32R) for i in range(2)]
        z2l = [sb(f"z2l{i}", [P, TG], F32R) for i in range(2)]
        wgt = [sb(f"wgt{i}", [P, GP, E]) for i in range(2)]
        wgtT = sb("wgtT", [E, GP, P])
        rt = sb("rt", [P, 8, GP, E])
        rq = sb("rq", [P, 8, GP])

        bank = [es.enter_context(nc.psum_tensor(f"bank{i}", [P, 512], F32)) for i in range(8)]
        ring = bank[0:RING]
        s_ps = bank[4:6]
        t_ps = bank[6]
        o_ps = bank[7]

        ld_w, ld_c, ld_m, ld_v, ld_e, ld_g = (sem(n) for n in ("ld_w", "ld_c", "ld_m", "ld_v", "ld_e", "ld_g"))
        consts, pro_t, pro_tc, pro_m, pro_h, pro_l = (
            sem(n) for n in ("consts", "pro_t", "pro_tc", "pro_m", "pro_h", "pro_l"))
        mrow_ok, mk_ps, mk_ok, cq_ok, vec_ps, vec_ok, w1_ok = (
            sem(n) for n in ("mrow_ok", "mk_ps", "mk_ok", "cq_ok", "vec_ps", "vec_ok", "w1_ok"))
        unit = sem("unit")
        act_ev = sem("act_ev")
        dve_ev = sem("dve_ev")
        c_hi = sem("c_hi")
        sc_ps = sem("sc_ps")
        sm_st = sem("sm_st")
        shifted = sem("shifted")
        exped = sem("exped")
        probs = sem("probs")
        t_full = sem("t_full")
        t_ev = sem("t_ev")
        att_ps = sem("att_ps")
        att_ok = sem("att_ok")
        st_ok = sem("st_ok")
        rs_ok = sem("rs_ok")
        z_ok = sem("z_ok")
        bo_ok = sem("bo_ok")
        f_unit, f_gelu, y_ps, y_add = (sem(n) for n in ("f_unit", "f_gelu", "y_ps", "y_add"))
        s1_ok, r1_ok, xp_ok, s2_ok, r2_ok, zn_ok, base_ok = (
            sem(n) for n in ("s1_ok", "r1_ok", "xp_ok", "s2_ok", "r2_ok", "zn_ok", "base_ok"))
        zt_ps, zt_ok, zl_ok, lg_ps, rt_ok, rd_ok, ex_ok = (
            sem(n) for n in ("zt_ps", "zt_ok", "zl_ok", "lg_ps", "rt_ok", "rd_ok", "ex_ok"))
        wt_ps, wt_ok, b_ps, b_ok, w_ok, stored = (
            sem(n) for n in ("wt_ps", "wt_ok", "b_ps", "b_ok", "w_ok", "stored"))

        block = es.enter_context(nc.Block())

        ROUTE_A, ROUTE_B = 3, 19

        @block.sync
        def _(sp):
            sp.dma_start(wq_s, Wq.rearrange("d (a n) -> d a n", a=2)).then_inc(ld_w, 16)
            sp.dma_start(wk_s, Wk.rearrange("d (a n) -> d a n", a=2)).then_inc(ld_w, 16)
            sp.dma_start(wv_s, Wv.rearrange("d (a n) -> d a n", a=2)).then_inc(ld_w, 16)
            sp.dma_start(wo_s, Wo.rearrange("(j p) n -> p j n", p=P)).then_inc(ld_w, 16)
            sp.dma_start(xs[:, 0:GP, :], x_t[:, 0:GP, :]).then_inc(ld_g, 16)
            sp.dma_start(c_in[:, :, :], c_t[:, 0:GP, :]).then_inc(ld_g, 16)
            sp.dma_start(w1_raw[:, :, :], W1.rearrange("e d f -> d e f")).then_inc(ld_e, 16)
            sp.dma_start(W2s[:, :, :, :], W2.rearrange("e (c p) n -> p e c n", p=P)).then_inc(ld_e, 16)
            with sp.Fori(1, NG) as g:
                sp.wait_ge(unit, units_done(g - 1, -1))
                sp.dma_start(xs[:, bass.ds(g * GP, GP), :], x_t[:, bass.ds(g * GP, GP), :]).then_inc(ld_g, 16)
                sp.dma_start(c_in[:, :, :], c_t[:, bass.ds(g * GP, GP), :]).then_inc(ld_g, 16)
            with sp.Fori(0, NG) as g:
                sp.wait_ge(y_add, (E * GP) * g + E * GP)
                sp.dma_start(out_t[:, bass.ds(g * GP, GP), :], xs[:, bass.ds(g * GP, GP), :]).then_inc(stored, 16)
            sp.wait_ge(stored, 16 * NG)

        @block.gpsimd
        def _(pool):
            pool.memset(ident[:, :], 0.0).then_inc(consts, 1)
            pool.memset(ident_b[:, :], 0.0).then_inc(consts, 1)
            pool.memset(causal[:, :], 0.0).then_inc(consts, 1)
            pool.memset(sel2[:, :], 1.0).then_inc(consts, 1)
            pool.memset(half[:, :], -0.5).then_inc(consts, 1)
            pool.memset(euler[:, :, :], EULER).then_inc(consts, 1)
            for e in range(E):
                pool.memset(rank[:, e:e + 1], float(E - e)).then_inc(consts, 1)
            pool.wait_ge(consts, 6 + E)
            pool.affine_select(out=ident[:, :], in_=ident[:, :], compare_op=ALU.not_equal, fill=1.0,
                               base=0, pattern=[[-1, P]], channel_multiplier=1).then_inc(consts, 1)
            pool.affine_select(out=ident_b[:, :], in_=ident_b[:, :], compare_op=ALU.not_equal, fill=1.0,
                               base=0, pattern=[[-1, P]], channel_multiplier=1).then_inc(consts, 1)
            pool.affine_select(out=causal[:, :], in_=causal[:, :], compare_op=ALU.is_ge, fill=NEG,
                               base=0, pattern=[[-1, P]], channel_multiplier=1).then_inc(consts, 1)
            pool.affine_select(out=sel2[:, :], in_=sel2[:, :], compare_op=ALU.is_ge, fill=0.0,
                               base=0, pattern=[[1, P]], channel_multiplier=-S).then_inc(consts, 1)
            pool.wait_ge(consts, 10 + E)
            pool.affine_select(out=sel2[:, :], in_=sel2[:, :], compare_op=ALU.is_ge, fill=0.0,
                               base=S - 1, pattern=[[-1, P]], channel_multiplier=S).then_inc(consts, 1)

            def prep(g):
                pool.wait_ge(st_ok, 9 * g + 9)
                pool.tensor_tensor(rs[:, :], ve[:, :], half[:, :], ALU.pow).then_inc(rs_ok, 1)
                pool.wait_ge(z_ok, GP * g + GP)
                pool.tensor_tensor(xs[:, bass.ds(g * GP, GP), :], xs[:, bass.ds(g * GP, GP), :],
                                   bo_b[:, :].unsqueeze(1).to_broadcast([P, GP, D]), ALU.add).then_inc(bo_ok, 1)

            pool.wait_ge(ld_v, 16 * 7)
            prep(0)
            pool.wait_ge(ld_e, 32)
            for e in range(0, E, 2):
                pool.tensor_copy(W1h[:, e:e + 2, :], w1_raw[:, e:e + 2, :]).then_inc(w1_ok, 1)
            for e in range(0, E, 2):
                pool.wait_ge(w1_ok, e // 2 + 1)
                pool.tensor_tensor(W1l[:, e:e + 2, :], w1_raw[:, e:e + 2, :], W1h[:, e:e + 2, :].bitcast(F32),
                                   ALU.subtract).then_inc(w1_ok, 1)
            with pool.Fori(1, NG) as g:
                prep(g)

            def moe_prep(g):
                pool.wait_ge(s1_ok, 9 * g + 9)
                pool.tensor_tensor(rs[:, :], ve[:, :], half[:, :], ALU.pow).then_inc(r1_ok, 1)
                pool.wait_ge(xp_ok, GP * g + GP)
                pool.wait_ge(s2_ok, 9 * g + 9)
                pool.tensor_tensor(rs[:, :], ve[:, :], half[:, :], ALU.pow).then_inc(r2_ok, 1)
                pool.tensor_tensor(xs[:, bass.ds(g * GP, GP), :], xs[:, bass.ds(g * GP, GP), :], xp,
                                   ALU.add).then_inc(base_ok, 1)
                pool.wait_ge(rt_ok, ROUTE_A * g + ROUTE_A)
                pool.tensor_tensor(rt[:, 1], euler[:, :, :], rt[:, 0], ALU.pow).then_inc(ex_ok, 1)

            with pool.Fori(0, NG) as g:
                moe_prep(g)

        @block.scalar
        def _(act):
            act.dma_start(mask_raw[:, :, :], mask.rearrange("(n two) s -> two n s", two=2)).then_inc(ld_m, 16)
            act.dma_start(vec_rows[0:E * FC, :], b1.rearrange("e (c p) -> (e c) p", p=P)).then_inc(ld_v, 16)
            act.dma_start(vec_rows[E * FC:E * FC + 1, :], ln_g.rearrange("(a d) -> a d", a=1)).then_inc(ld_v, 16)
            act.dma_start(vec_rows[E * FC + 1:E * FC + 2, :], ln_b.rearrange("(a d) -> a d", a=1)).then_inc(ld_v, 16)
            act.dma_start(bo_b[:, :], bo.rearrange("(a d) -> a d", a=1).to_broadcast([P, D])).then_inc(ld_v, 16)
            act.dma_start(rb_b[:, :], rb.rearrange("(a d) -> a d", a=1).to_broadcast([P, E])).then_inc(ld_v, 16)
            act.dma_start(rW_s[:, :], rW).then_inc(ld_v, 16)
            act.dma_start(b2_s[:, :], b2).then_inc(ld_v, 16)

            for k in range(3):
                act.wait_ge(pro_t, k + 1)
                act.activation(wT[:, k // 2, 4 * (k % 2):4 * (k % 2) + 4, :],
                               bank[k].rearrange("p (j n) -> p j n", n=P), ACT.Copy).then_inc(pro_tc, 1)
            Ap = Ah[:, :, :].rearrange("p (q two) d -> p two q d", two=2)
            for k in range(8):
                act.wait_ge(pro_m, k + 1)
                src = bank[k].rearrange("p (j n) -> p j n", n=D)
                if k < 4:
                    act.activation(Ap[:, k // 2, 4 * (k % 2):4 * (k % 2) + 4, :], src, ACT.Copy,
                                   scale=DH ** -0.5).then_inc(pro_h, 1)
                else:
                    act.activation(Nh[:, (k - 4) // 2, 4 * (k % 2):4 * (k % 2) + 4, :], src,
                                   ACT.Copy).then_inc(pro_h, 1)

            def prep_units(g):
                base = KEY_UNITS + VALUE_UNITS
                for k in range(2):
                    act.wait_ge(unit, units_done(g, base + k))
                    act.activation(zT[:, 256 * k:256 * k + 256], ring[k][:, 0:256], ACT.Copy).then_inc(act_ev, 1)
                for k in range(2):
                    act.wait_ge(unit, units_done(g, base + 2 + k))
                    act.activation(cTh[:, 256 * k:256 * k + 256], ring[2 + k][:, 0:256],
                                   ACT.Copy).then_inc(act_ev, 1)

            def t_unit(n, par, t):
                act.wait_ge(t_full, 2 * n + t + 1)
                if not (isinstance(n, int) and n == 0):
                    act.wait_ge(att_ps, 2 * n + t - 1)
                act.activation(pT[:, 4 * t:4 * t + 4, :], t_ps.rearrange("p (j n) -> p j n", n=P),
                               ACT.Copy).then_inc(t_ev, 1)

            def exp_half(n, par, t):
                act.wait_ge(shifted, 2 * n + t + 1)
                act.activation(pr[par][:, 8 * t:8 * t + 8, :], pr[par][:, 8 * t:8 * t + 8, :],
                               ACT.Exp).then_inc(exped, 1)

            def group(g, first=False, last=False):
                for idx in range(0, KEY_UNITS, 2):
                    act.wait_ge(unit, units_done(g, idx))
                    act.activation(kf[:, idx, :], ring[idx % RING][:, :], ACT.Copy).then_inc(act_ev, 1)
                    if not first and idx in (2, 6):
                        t_unit(GP * g - 1, 1, (idx - 2) // 4)
                for i in range(GP):
                    n, par = GP * g + i, i % 2
                    for k in range(4):
                        idx = KEY_UNITS + 4 * i + k
                        act.wait_ge(unit, units_done(g, idx))
                        if k == 0 and not (first and i < 2):
                            act.wait_ge(att_ps, 2 * n - 2)
                        par_h, q4 = k // 2, k % 2
                        for b in range(2):
                            act.activation(vf[par][64 * par_h:64 * par_h + 64, b, 4 * q4:4 * q4 + 4, :],
                                           ring[idx % RING][64 * b:64 * b + 64, :].rearrange(
                                               "p (j n) -> p j n", n=D), ACT.Copy).then_inc(act_ev, 1)
                        if k == 0:
                            if i > 0:
                                t_unit(n - 1, 1 - par, 0)
                            exp_half(n, par, 0)
                        if k == 1:
                            exp_half(n, par, 1)
                            if i > 0:
                                t_unit(n - 1, 1 - par, 1)
                if not last:
                    prep_units(g)

            prep_units(-1)
            group(0, first=True)
            with act.Fori(1, NG - 1) as g:
                group(g)
            group(NG - 1, last=True)
            for t in range(2):
                t_unit(NP - 1, 1, t)

            def zt_evac(g, par):
                act.wait_ge(zt_ps, g + 1)
                act.activation(z2T[par], t_ps[:, :], ACT.Identity, bias=bc, scale=gc).then_inc(zt_ok, 1)
                act.activation(z2h[par][:, :], t_ps[:, :], ACT.Identity, bias=bc, scale=gc).then_inc(zt_ok, 1)

            def moe_group(g, par, last=False):
                for u in range(E * FC):
                    act.wait_ge(f_unit, E * FC * g + u + 1)
                    if u >= 4 or not (isinstance(g, int) and g == 0):
                        act.wait_ge(y_ps, E * g + u // FC - 1)
                    act.activation(hid[u % 4], ring[u % RING][:, :], ACT.Gelu,
                                   bias=b1c[:, u:u + 1]).then_inc(f_gelu, 1)
                    if u == 10 and not last:
                        zt_evac(g + 1, 1 - par)

            act.wait_ge(vec_ok, 1)
            act.wait_ge(att_ps, 2 * NP)
            zt_evac(0, 0)
            moe_group(0, 0)
            moe_group(1, 1)
            with act.Fori(1, NG // 2 - 1) as gg:
                moe_group(2 * gg, 0)
                moe_group(2 * gg + 1, 1)
            moe_group(NG - 2, 0)
            moe_group(NG - 1, 1, last=True)

        @block.tensor
        def _(pe):
            def split_product(ps, lh, ll, rh, rl):
                pe.matmul(ps, lh, rh, start=True, stop=False)
                pe.matmul(ps, lh, rl, start=False, stop=False)
                return pe.matmul(ps, ll, rh, start=False, stop=True)

            pe.wait_ge(consts, 11 + E)
            pe.wait_ge(ld_w, 64)
            for k in range(6):
                w = (wq_s, wk_s, wv_s)[k // 2]
                for j in range(4):
                    last = pe.transpose(bank[k][:, j * P:(j + 1) * P], w[:, k % 2, j * P:(j + 1) * P], ident[:, :])
                last.then_inc(pro_t, 1)
            pe.wait_ge(ld_v, 16 * 7)
            pe.transpose(bank[7][:, 0:E * FC + 2], vec_rows[:, :], ident[0:E * FC + 2, 0:E * FC + 2]).then_inc(vec_ps, 1)
            pe.wait_ge(pro_tc, 6)
            pe.wait_ge(vec_ok, 1)
            for k in range(8):
                hp, q4 = (k // 2) % 2, k % 2
                rows = slice(64 * hp, 64 * hp + 64)
                for q in range(4):
                    j = 4 * q4 + q
                    lhs = wT[rows, 1, j, :] if k < 4 else wT[rows, 2, j, :]
                    rhs = wT[rows, 0, j, :] if k < 4 else wo_s[rows, j, :]
                    last = pe.matmul(bank[k][:, q * D:(q + 1) * D], lhs, rhs, start=True, stop=True)
                last.then_inc(pro_m, 1)
            pe.wait_ge(mrow_ok, 2)
            for k in range(8):
                pe.wait_ge(pro_l, k + 1)
                pe.matmul(bank[k][:, :].rearrange("p (n s) -> p n s", s=S), sel2[:, :],
                          mask_row[:, 8 * k:8 * k + 8, :], start=True, stop=True).then_inc(mk_ps, 1)
            pe.wait_ge(mk_ok, 8)

            def ring_free(g, idx):
                a, d = unit_owner((idx - RING) % UNITS)
                if d:
                    pe.wait_ge(dve_ev, dve_done(g, idx - RING))
                else:
                    pe.wait_ge(act_ev, act_done(g, idx - RING))

            def prep_units(g, free=True):
                base = KEY_UNITS + VALUE_UNITS
                for k in range(4):
                    if free:
                        ring_free(g, base + k)
                    if k == 0:
                        pe.wait_ge(z_ok, GP * (g + 1) + GP)
                    if k == 2:
                        pe.wait_ge(ld_g, 32 * (g + 1) + 32)
                    for t in range(2):
                        tile = 2 * (k % 2) + t
                        src = z[:, tile, :] if k < 2 else c_in[:, tile, :]
                        last = pe.transpose(ring[k][:, t * P:(t + 1) * P], src, ident[:, :])
                    last.then_inc(unit, 1)

            def t_half(n, par, t):
                pe.wait_ge(probs, 2 * n + t + 1)
                if t == 1 or not (isinstance(n, int) and n == 0):
                    pe.wait_ge(t_ev, 2 * n + t)
                for q in range(4):
                    j = 4 * t + q
                    last = pe.transpose(t_ps[:, q * P:(q + 1) * P],
                                        pr[par][:, 2 * j:2 * j + 2, :].rearrange("p a s -> p (a s)"), ident[:, :])
                last.then_inc(t_full, 1)

            def attend(n, par, t):
                pe.wait_ge(t_ev, 2 * n + t + 1)
                if t == 0 and not (isinstance(n, int) and n == 0):
                    pe.wait_ge(att_ok, n)
                for j in range(4 * t, 4 * t + 4):
                    for b in range(2):
                        last = pe.matmul(o_ps[64 * b:64 * b + 64, 0:D], pT[:, j, 64 * b:64 * b + 64],
                                         vf[par][:, b, j, :], start=(j == 0), stop=(j == H // 2 - 1),
                                         skip_group_check=True)
                last.then_inc(att_ps, 1)

            def scores(g, i, hf):
                n = GP * g + i
                if True:
                    if not (isinstance(n, int) and n == 0):
                        pe.wait_ge(shifted, 2 * n + hf - 1)
                    heads = s_ps[hf][:, :].rearrange("p (h s) -> p h s", s=S)
                    mrow = mask_b[:, n, :].unsqueeze(1).to_broadcast([P, 8, S])
                    pe.matmul(heads, ident_b[:, :], mrow, start=True, stop=False, skip_group_check=True)
                    for b in range(2):
                        cols = slice(i * P + 64 * b, i * P + 64 * b + 64)
                        last = pe.matmul(heads[64 * b:64 * b + 64], zT[:, cols], kf[:, 8 * hf:8 * hf + 8, cols],
                                         start=False, stop=True, skip_group_check=True)
                    last.then_inc(sc_ps, 1)

            def value_unit(g, i, k):
                idx = KEY_UNITS + 4 * i + k
                ring_free(g, idx)
                toks = slice(i * P, (i + 1) * P)
                heads = (slice(None), k // 2, slice(4 * (k % 2), 4 * (k % 2) + 4), slice(None))
                split_product(ring[idx % RING][:, :].rearrange("p (j n) -> p j n", n=D),
                              cTh[:, toks], cTl[:, toks], Nh[heads], Nl[heads]).then_inc(unit, 1)

            def group(g, first=False, last=False):
                pe.wait_ge(dve_ev, dve_done(g, -1))
                for idx in range(KEY_UNITS):
                    ring_free(g, idx)
                    split_product(ring[idx % RING][:, :], Ah[:, idx, :], Al[:, idx, :],
                                  cTh[:, :], cTl[:, :]).then_inc(unit, 1)
                    if not first:
                        if idx == 3:
                            t_half(GP * g - 1, 1, 0)
                        if idx == 6:
                            attend(GP * g - 1, 1, 0)
                            t_half(GP * g - 1, 1, 1)
                        if idx == 9:
                            attend(GP * g - 1, 1, 1)
                pe.wait_ge(act_ev, act_done(g, KEY_UNITS - 1))
                pe.wait_ge(dve_ev, dve_done(g, KEY_UNITS - 1))
                for i in range(GP):
                    n, par = GP * g + i, i % 2
                    scores(g, i, 0)
                    value_unit(g, i, 0)
                    scores(g, i, 1)
                    if i == 0:
                        for k in range(1, 4):
                            value_unit(g, i, k)
                        continue
                    t_half(n - 1, 1 - par, 0)
                    value_unit(g, i, 1)
                    pe.wait_ge(act_ev, act_done(g, KEY_UNITS + 4 * i - 1))
                    if i < GP - 1:
                        attend(n - 1, 1 - par, 0)
                        t_half(n - 1, 1 - par, 1)
                        value_unit(g, i, 2)
                        attend(n - 1, 1 - par, 1)
                        value_unit(g, i, 3)
                    else:
                        t_half(n - 1, 1 - par, 1)
                        value_unit(g, i, 2)
                        value_unit(g, i, 3)
                        if not last:
                            prep_units(g)
                        attend(n - 1, 1 - par, 0)
                        attend(n - 1, 1 - par, 1)

            prep_units(-1, free=False)
            group(0, first=True)
            with pe.Fori(1, NG - 1) as g:
                group(g)
            group(NG - 1, last=True)
            for t in range(2):
                t_half(NP - 1, 1, t)
            pe.wait_ge(act_ev, act_done(NG - 1, KEY_UNITS + VALUE_UNITS - 1))
            attend(NP - 1, 1, 0)
            attend(NP - 1, 1, 1)

            y_bank = s_ps
            lg_bank = o_ps

            def z_transposes(g):
                pe.wait_ge(zn_ok, GP * g + GP)
                if not (isinstance(g, int) and g == 0):
                    pe.wait_ge(b_ok, g)
                for t in range(GP):
                    last = pe.transpose(t_ps[:, t * P:(t + 1) * P], zn[:, t, :], ident[:, :])
                last.then_inc(zt_ps, 1)

            def logits(g, par):
                pe.wait_ge(zt_ok, 2 * g + 1)
                if not (isinstance(g, int) and g == 0):
                    pe.wait_ge(wt_ok, g)
                for t in range(GP):
                    last = pe.matmul(lg_bank[:, t * E:(t + 1) * E], z2T[par][:, t * P:(t + 1) * P], rW_s[:, :],
                                     start=True, stop=True)
                last.then_inc(lg_ps, 1)

            def weights_t(g, par):
                pe.wait_ge(w_ok, g + 1)
                for t in range(GP):
                    last = pe.transpose(lg_bank[0:E, t * P:(t + 1) * P], wgt[par][:, t, :], ident[:, :])
                last.then_inc(wt_ps, 1)

            def b2_part(g):
                pe.wait_ge(wt_ok, g + 1)
                for t in range(GP):
                    last = pe.matmul(t_ps[:, t * D:(t + 1) * D], wgtT[:, t, :], b2_s[:, :], start=True, stop=True)
                last.then_inc(b_ps, 1)

            def up(g, par, u):
                if u >= RING or not (isinstance(g, int) and g == 0):
                    pe.wait_ge(f_gelu, E * FC * g + u + 1 - RING)
                e, fc = u // FC, u % FC
                cols = slice(fc * P, (fc + 1) * P)
                split_product(ring[u % RING][:, :], W1h[:, e, cols], W1l[:, e, cols],
                              z2h[par][:, :], z2l[par][:, :]).then_inc(f_unit, 1)

            def down(g, e):
                pe.wait_ge(f_gelu, E * FC * g + FC * (e + 1))
                if e >= 2 or not (isinstance(g, int) and g == 0):
                    pe.wait_ge(y_add, GP * (E * g + e - 1))
                for t in range(GP):
                    for fc in range(FC):
                        last = pe.matmul(y_bank[e % 2][:, t * D:(t + 1) * D],
                                         hid[(FC * e + fc) % 4][:, t * P:(t + 1) * P], W2s[:, e, fc, :],
                                         start=(fc == 0), stop=(fc == FC - 1))
                last.then_inc(y_ps, 1)

            def moe_group(g, par, last=False):
                pe.wait_ge(zl_ok, g + 1)
                for e in range(E):
                    for fc in range(FC):
                        up(g, par, FC * e + fc)
                    if e > 0:
                        down(g, e - 1)
                    if e == 1:
                        weights_t(g, par)
                    if e == 2:
                        b2_part(g)
                    if e == 4 and not last:
                        z_transposes(g + 1)
                    if e == 5 and not last:
                        logits(g + 1, 1 - par)
                down(g, E - 1)

            pe.wait_ge(att_ok, NP)
            pe.wait_ge(w1_ok, E)
            pe.wait_ge(ld_e, 32)
            z_transposes(0)
            logits(0, 0)
            moe_group(0, 0)
            moe_group(1, 1)
            with pe.Fori(1, NG // 2 - 1) as gg:
                moe_group(2 * gg, 0)
                moe_group(2 * gg + 1, 1)
            moe_group(NG - 2, 0)
            moe_group(NG - 1, 1, last=True)

        @block.vector
        def _(dve):
            for k in range(3, 6):
                dve.wait_ge(pro_t, k + 1)
                dve.tensor_copy(wT[:, k // 2, 4 * (k % 2):4 * (k % 2) + 4, :],
                                bank[k].rearrange("p (j n) -> p j n", n=P)).then_inc(pro_tc, 1)
            dve.wait_ge(vec_ps, 1)
            dve.tensor_copy(vec_cols[:, :], bank[7][:, 0:E * FC + 2]).then_inc(vec_ok, 1)
            dve.wait_ge(ld_m, 16)
            for k in range(2):
                dve.tensor_scalar(mask_row[:, 32 * k:32 * k + 32, :], mask_raw[:, 32 * k:32 * k + 32, :], NEG, None,
                                  ALU.mult).then_inc(mrow_ok, 1)
            dve.wait_ge(consts, 11 + E)
            for b in range(2):
                dve.tensor_copy(causal_q[64 * b:64 * b + 64, :],
                                causal[64 * b:64 * b + 64, 64 * b:64 * b + 64]).then_inc(cq_ok, 1)
            Ahp = Ah[:, :, :].rearrange("p (q two) d -> p two q d", two=2)
            Alp = Al[:, :, :].rearrange("p (q two) d -> p two q d", two=2)
            for k in range(8):
                dve.wait_ge(pro_h, k + 1)
                src = bank[k].rearrange("p (j n) -> p j n", n=D)
                js = slice(4 * (k % 2), 4 * (k % 2) + 4)
                if k < 4:
                    dve.scalar_tensor_tensor(out=Alp[:, k // 2, js, :], in0=src, scalar=DH ** -0.5,
                                             in1=Ahp[:, k // 2, js, :].bitcast(F32), op0=ALU.mult,
                                             op1=ALU.subtract).then_inc(pro_l, 1)
                else:
                    dve.tensor_tensor(Nl[:, (k - 4) // 2, js, :], src, Nh[:, (k - 4) // 2, js, :].bitcast(F32),
                                      ALU.subtract).then_inc(pro_l, 1)
            dve.wait_ge(cq_ok, 2)
            for k in range(8):
                dve.wait_ge(mk_ps, k + 1)
                dve.tensor_tensor(mask_b[:, 8 * k:8 * k + 8, :], bank[k].rearrange("p (n s) -> p n s", s=S),
                                  causal_q[:, :].unsqueeze(1).to_broadcast([P, 8, S]), ALU.min).then_inc(mk_ok, 1)

            def norm_stats(src, done, g):
                for t in range(GP):
                    dve.bn_stats(st[:, t, :], src(t)).then_inc(done, 1)
                dve.wait_ge(done, 9 * g + 4)
                dve.memset(idle[:, :], 0.0)
                for t in range(GP):
                    dve.bn_aggr(mv[:, t, :], st[:, t, :]).then_inc(done, 1)
                dve.wait_ge(done, 9 * g + 8)
                dve.tensor_scalar(ve[:, :], mv[:, :, 1], LN_EPS, None, ALU.add).then_inc(done, 1)

            def prep_stats(g):
                dve.wait_ge(ld_g, 32 * g + 32)
                norm_stats(lambda t: xs[:, g * GP + t, :], st_ok, g)

            def prep_z(g, tiles):
                dve.wait_ge(rs_ok, g + 1)
                for t in tiles:
                    dve.tensor_scalar(z[:, t, :], xs[:, g * GP + t, :], mv[:, t, 0:1], rs[:, t:t + 1],
                                      ALU.subtract, ALU.mult).then_inc(z_ok, 1)

            def prep_units(g):
                base = KEY_UNITS + VALUE_UNITS
                for k in range(2):
                    dve.wait_ge(act_ev, act_done(g, base + 2 + k))
                    dve.tensor_tensor(cTl[:, 256 * k:256 * k + 256], ring[2 + k][:, 0:256],
                                      cTh[:, 256 * k:256 * k + 256].bitcast(F32), ALU.subtract).then_inc(dve_ev, 1)

            def add_attention(n):
                dve.wait_ge(att_ps, 2 * n + 2)
                dve.tensor_tensor(xs[:, n, :], o_ps[:, 0:D], xs[:, n, :], ALU.add).then_inc(att_ok, 1)

            def shift_half(n, par, t):
                hs = slice(8 * t, 8 * t + 8)
                src = s_ps[t][:, :].rearrange("p (h s) -> p h s", s=S)
                dve.wait_ge(sc_ps, 2 * n + t + 1)
                dve.reduce_max(mx[:, par, hs], src, AX_X).then_inc(sm_st, 1)
                dve.wait_ge(sm_st, 6 * n + t + 1)
                dve.tensor_tensor(pr[par][:, hs, :], src, mx[:, par, hs].unsqueeze(2).to_broadcast([P, 8, S]),
                                  ALU.subtract).then_inc(shifted, 1)

            def normalize_half(n, par, t):
                hs = slice(8 * t, 8 * t + 8)
                dve.wait_ge(exped, 2 * n + t + 1)
                dve.reduce_sum(sm[:, par, hs], pr[par][:, hs, :], AX_X).then_inc(sm_st, 1)
                dve.wait_ge(sm_st, 6 * n + 2 * t + 3)
                dve.reciprocal(ri[:, par, hs], sm[:, par, hs]).then_inc(sm_st, 1)
                dve.wait_ge(sm_st, 6 * n + 2 * t + 4)
                dve.tensor_tensor(pr[par][:, hs, :], pr[par][:, hs, :],
                                  ri[:, par, hs].unsqueeze(2).to_broadcast([P, 8, S]), ALU.mult).then_inc(probs, 1)

            def group(g, first=False, last=False):
                if not first:
                    add_attention(GP * g - 2)
                for idx in range(1, KEY_UNITS, 2):
                    dve.wait_ge(unit, units_done(g, idx))
                    dve.tensor_copy(kf[:, idx, :], ring[idx % RING][:, :]).then_inc(dve_ev, 1)
                    if not last and idx == 9:
                        prep_stats(g + 1)
                    if not last and idx in (13, 15):
                        prep_z(g + 1, (idx - 13, idx - 12))
                for i in range(GP):
                    n, par = GP * g + i, i % 2
                    if not (first and i < 2):
                        dve.wait_ge(t_full, 2 * n - 2)
                    shift_half(n, par, 0)
                    shift_half(n, par, 1)
                    if i == 0:
                        if not first:
                            add_attention(GP * g - 1)
                        dve.wait_ge(bo_ok, g + 1)
                    elif i > 1:
                        add_attention(n - 2)
                    normalize_half(n, par, 0)
                    normalize_half(n, par, 1)
                if not last:
                    prep_units(g)

            prep_stats(0)
            prep_z(0, range(GP))
            prep_units(-1)
            group(0, first=True)
            with dve.Fori(1, NG - 1) as g:
                group(g)
            group(NG - 1, last=True)
            add_attention(NP - 2)
            add_attention(NP - 1)

            def x_norm(g):
                dve.wait_ge(r1_ok, g + 1)
                for t in range(GP):
                    dve.tensor_scalar(xp[:, t, :], xs[:, g * GP + t, :], mv[:, t, 0:1], rs[:, t:t + 1],
                                      ALU.subtract, ALU.mult).then_inc(xp_ok, 1)
                dve.wait_ge(xp_ok, GP * g + GP)

            def z_norm(g):
                dve.wait_ge(r2_ok, g + 1)
                for t in range(GP):
                    dve.tensor_scalar(zn[:, t, :], xp[:, t, :], mv[:, t, 0:1], rs[:, t:t + 1],
                                      ALU.subtract, ALU.mult).then_inc(zn_ok, 1)

            def z_low(g, par):
                dve.wait_ge(zt_ok, 2 * g + 2)
                dve.tensor_tensor(z2l[par][:, :], z2T[par], z2h[par][:, :].bitcast(F32),
                                  ALU.subtract).then_inc(zl_ok, 1)

            def route_a(g):
                def step(ins, k):
                    ins.then_inc(rt_ok, 1)
                    dve.wait_ge(rt_ok, ROUTE_A * g + k)
                dve.wait_ge(lg_ps, g + 1)
                step(dve.tensor_tensor(rt[:, 2], o_ps[:, 0:GP * E].rearrange("p (t e) -> p t e", e=E),
                                       rb_b[:, :].unsqueeze(1).to_broadcast([P, GP, E]), ALU.add), 1)
                step(dve.reduce_max(rq[:, 0], rt[:, 2], AX_X), 2)
                step(dve.tensor_tensor(rt[:, 0], rt[:, 2], rq[:, 0].unsqueeze(2).to_broadcast([P, GP, E]),
                                       ALU.subtract), 3)

            def route_b(g, par):
                count = [0]

                def step(ins):
                    count[0] += 1
                    ins.then_inc(rd_ok, 1)
                    dve.wait_ge(rd_ok, ROUTE_B * g + count[0])

                def wide(a):
                    return a.unsqueeze(2).to_broadcast([P, GP, E])

                ranks = rank[:, :].unsqueeze(1).to_broadcast([P, GP, E])
                dve.wait_ge(ex_ok, g + 1)
                step(dve.reduce_sum(rq[:, 1], rt[:, 1], AX_X))
                step(dve.reciprocal(rq[:, 2], rq[:, 1]))
                step(dve.tensor_tensor(rt[:, 2], rt[:, 1], wide(rq[:, 2]), ALU.mult))
                p = rt[:, 2]
                for k in range(2):
                    step(dve.reduce_max(rq[:, 3], p, AX_X))
                    step(dve.tensor_tensor(rt[:, 3], p, wide(rq[:, 3]), ALU.is_equal))
                    step(dve.tensor_tensor(rt[:, 3], rt[:, 3], ranks, ALU.mult))
                    step(dve.reduce_max(rq[:, 4], rt[:, 3], AX_X))
                    step(dve.tensor_tensor(rt[:, 4 + k], ranks, wide(rq[:, 4]), ALU.is_equal))
                    if k == 0:
                        step(dve.scalar_tensor_tensor(out=rt[:, 6], in0=rt[:, 4], scalar=-2.0, in1=p,
                                                      op0=ALU.mult, op1=ALU.add))
                        p = rt[:, 6]
                step(dve.tensor_tensor(rt[:, 7], rt[:, 4], rt[:, 5], ALU.add))
                step(dve.tensor_tensor(rt[:, 7], rt[:, 7], rt[:, 2], ALU.mult))
                step(dve.reduce_sum(rq[:, 5], rt[:, 7], AX_X))
                step(dve.tensor_scalar(rq[:, 5], rq[:, 5], 1e-8, None, ALU.max))
                step(dve.reciprocal(rq[:, 6], rq[:, 5]))
                dve.tensor_tensor(wgt[par][:, :, :], rt[:, 7], wide(rq[:, 6]), ALU.mult).then_inc(w_ok, 1)
                assert count[0] == ROUTE_B

            def combine(g, par, e):
                dve.wait_ge(y_ps, E * g + e + 1)
                if e > 0:
                    dve.wait_ge(y_add, GP * (E * g + e))
                for t in range(GP):
                    dve.scalar_tensor_tensor(out=xs[:, g * GP + t, :], in0=s_ps[e % 2][:, t * D:(t + 1) * D],
                                             scalar=wgt[par][:, t, e:e + 1], in1=xs[:, g * GP + t, :],
                                             op0=ALU.mult, op1=ALU.add).then_inc(y_add, 1)

            def moe_group(g, par, last=False):
                if not last:
                    norm_stats(lambda t: xs[:, (g + 1) * GP + t, :], s1_ok, g + 1)
                dve.wait_ge(base_ok, g + 1)
                dve.wait_ge(w_ok, g + 1)
                for e in range(E):
                    combine(g, par, e)
                    if e == 0:
                        dve.wait_ge(wt_ps, g + 1)
                        dve.tensor_copy(wgtT[:, :, :], o_ps[0:E, :].rearrange("e (t p) -> e t p", p=P)).then_inc(wt_ok, 1)
                        if not last:
                            x_norm(g + 1)
                            norm_stats(lambda t: xp[:, t, :], s2_ok, g + 1)
                    if e == 2 and not last:
                        z_norm(g + 1)
                    if e == 1:
                        dve.wait_ge(b_ps, g + 1)
                        dve.wait_ge(y_add, E * GP * g + (e + 1) * GP)
                        dve.tensor_tensor(xs[:, bass.ds(g * GP, GP), :],
                                          t_ps[:, :].rearrange("p (t d) -> p t d", d=D),
                                          xs[:, bass.ds(g * GP, GP), :], ALU.add).then_inc(b_ok, 1)
                        dve.wait_ge(b_ok, g + 1)
                    if e == 3 and not last:
                        z_low(g + 1, 1 - par)
                    if e == 4 and not last:
                        route_a(g + 1)
                    if e == 6 and not last:
                        route_b(g + 1, 1 - par)

            norm_stats(lambda t: xs[:, t, :], s1_ok, 0)
            x_norm(0)
            norm_stats(lambda t: xp[:, t, :], s2_ok, 0)
            z_norm(0)
            z_low(0, 0)
            route_a(0)
            route_b(0, 0)
            moe_group(0, 0)
            moe_group(1, 1)
            with dve.Fori(1, NG // 2 - 1) as gg:
                moe_group(2 * gg, 0)
                moe_group(2 * gg + 1, 1)
            moe_group(NG - 2, 0)
            moe_group(NG - 1, 1, last=True)


_INS = ['x', 'ctx_1024', 'mask_BxS2_bf0', 'L0_xattn_Wq', 'L0_xattn_Wk', 'L0_xattn_Wv', 'L0_xattn_Wo', 'L0_xattn_bo',
        'L0_ffn_ln_g', 'L0_ffn_ln_b', 'L0_ffn_rW', 'L0_ffn_rb', 'L0_ffn_W1', 'L0_ffn_b1', 'L0_ffn_W2', 'L0_ffn_b2']
_OUTS = [((128, 64, 128), 'float32')]


def kernel(**inputs):
    import numpy as _np
    import concourse.bacc as _bacc
    from concourse import mybir as _mybir
    from concourse.bass_utils import run_bass_kernel_spmd as _run

    nc = _bacc.Bacc("TRN2", target_bir_lowering=False, num_devices=1)
    arrays, args = {}, []
    for name in _INS:
        a = _np.ascontiguousarray(inputs[name])
        arrays[f"in_{name}_dram"] = a
        args.append(nc.dram_tensor(f"in_{name}_dram", a.shape, _mybir.dt.from_np(a.dtype), kind="ExternalInput").ap())
    for i, (shape, dtype) in enumerate(_OUTS):
        dt = _mybir.dt.from_np(_np.dtype(dtype))
        args.append(nc.dram_tensor(f"out_{i}_dram", shape, dt, kind="ExternalOutput").ap())
    xattn_ffn_kernel(nc, *args)
    r = _run(nc, [arrays], core_ids=[0])
    got = tuple(r.results[0][f"out_{i}_dram"] for i in range(len(_OUTS)))
    return got[0]
```

```python
from contextlib import ExitStack

import concourse.bass as bass
from concourse import mybir

F32 = mybir.dt.float32
F32R = mybir.dt.float32r
BF16 = mybir.dt.bfloat16
U8 = mybir.dt.uint8
I32 = mybir.dt.int32
ALU = mybir.AluOpType
ACT = mybir.ActivationFunctionType
AX_X = mybir.AxisListType.X

P = 128
LN_EPS = 1e-5
NEG = -3.3895313892515355e38
TILE = 256
PAD_TOKEN = 20000.0

RING = 4
KEYS = [f"K{h}" for h in range(16)]
PREP = ["ZA", "ZB", "CA", "CB"]


def values(i):
    return [f"V{i}{k}" for k in range(4)]


ORDER_FIRST = KEYS + values(0) + values(1) + values(2) + values(3) + PREP
ORDER = (KEYS + values(0) + values(1)[:1] + ["RA", "RB"] + values(1)[1:2] + ["RL"] + values(1)[2:]
         + values(2)[:2] + ["RX"] + values(2)[2:] + values(3) + PREP)
assert len(ORDER) % RING == 0 and len(ORDER_FIRST) % RING == 0


def unit_owner(name):
    if name[0] == "K":
        return (0, 1) if int(name[1:]) % 4 == 3 else (1, 0)
    if name[0] == "V":
        return (2, 0)
    return {"RA": (1, 0), "RB": (1, 0), "RL": (0, 1), "RX": (0, 1),
            "ZA": (1, 0), "ZB": (1, 0), "CA": (1, 1), "CB": (1, 1)}[name]


def total(order, who=None):
    return len(order) if who is None else sum(unit_owner(name)[who] for name in order)


class Group:

    def __init__(self, order, started, before):
        self.order, self.started, self.before = order, started, before

    def _count(self, who, n):
        if not self.started:
            return total(PREP + self.order[:n], who) if self.order is not PREP else total(self.order[:n], who)
        return total(PREP + ORDER_FIRST, who) + total(ORDER, who) * self.before + total(self.order[:n], who)

    def done(self, name, who=None):
        return self._count(who, self.order.index(name) + 1)

    def freed(self, name):
        n = self.order.index(name) - RING
        before = self.order[n] if n >= 0 else PREP[n]
        who = 1 if unit_owner(before)[1] else 0
        if n >= 0:
            return who, self._count(who, n + 1)
        return who, self._count(who, 0) - total(PREP[len(PREP) + n + 1:], who)

    def bank(self, name):
        return self.order.index(name) % RING


def xattn_ffn_kernel(nc, x, ctx_in, mask, Wq, Wk, Wv, Wo, bo, ln_g, ln_b, rW, rb, W1, b1, W2, b2, out):
    B, S, D = x.shape
    INNER = Wq.shape[1]
    DH = 64
    H = INNER // DH
    E, _, HF = W1.shape
    FC = HF // P
    NP = B * S // P
    GP = 4
    NG = NP // GP
    TG = GP * P
    NTOK = B * S
    REGION = NTOK + TILE
    NB_MAX = NTOK // TILE
    NT = 2 * NTOK // TILE + E
    assert S == 64 and D == P and H == 16 and E == 8 and FC == 2 and NG == 16 and NT % 8 == 0

    x_t = x.rearrange("(n two) s d -> (two s) n d", two=2)
    c_t = ctx_in.rearrange("(n two) s d -> (two s) n d", two=2)
    out_t = out.rearrange("(n two) s d -> (two s) n d", two=2)

    CONSTS = 10 + 2 * E + 3 + 7
    TAB_NEXT, TAB_ALL = 1, 19

    with ExitStack() as es:
        def sb(name, shape, dt=F32):
            return es.enter_context(nc.sbuf_tensor(name, shape, dt))

        def sem(name):
            return es.enter_context(nc.semaphore(name))

        xs = sb("xs", [P, NP, D])
        c_in = sb("c_in", [P, GP, D])
        z = sb("z", [P, GP, D])
        zT = sb("zT", [P, TG])
        cTh = sb("cTh", [P, TG], F32R)
        cTl = sb("cTl", [P, TG], F32R)
        Ah = sb("Ah", [P, H, D], F32R)
        Al = sb("Al", [P, H, D], F32R)
        Nh = sb("Nh", [P, 2, H // 2, D], F32R)
        Nl = sb("Nl", [P, 2, H // 2, D], F32R)
        kf = sb("kf", [P, H, TG])
        vf = [sb(f"vf{i}", [P, 2, H // 2, D]) for i in range(2)]
        pr = [sb(f"pr{i}", [P, H, S]) for i in range(2)]
        pT = sb("pT", [P, H // 2, P])
        mask_b = sb("mask_b", [P, NP, S], BF16)
        B1, B2 = FC * D, FC * D + FC
        experts = sb("experts", [P, E, 2 * HF + B2 + D])
        upper_b = sb("upper_b", [P, P], BF16)
        ones_b = sb("ones_b", [P, P], BF16)
        ones_row = sb("ones_row", [1, P])
        ident = sb("ident", [P, P])
        ident_b = sb("ident_b", [P, P], BF16)
        causal = sb("causal", [P, P])
        causal_q = sb("causal_q", [P, S])
        sel2 = sb("sel2", [2, P], BF16)
        bo_b = sb("bo_b", [P, D])
        rb_b = sb("rb_b", [P, E])
        rW_s = sb("rW_s", [P, E])
        vec_rows = sb("vec_rows", [E * FC + 2, P])
        vec_cols = sb("vec_cols", [P, E * FC + 2])
        b1c = vec_cols[:, 0:E * FC]
        gc = vec_cols[:, E * FC:E * FC + 1]
        bc = vec_cols[:, E * FC + 1:E * FC + 2]
        bc_wide = sb("bc_wide", [P, P])
        b1_sum = sb("b1_sum", [P, E * FC])
        rW_g = sb("rW_g", [P, E])
        rb_sum = sb("rb_sum", [P, E])
        rank = sb("rank", [P, E])
        region = sb("region", [P, E])
        half = sb("half", [P, GP])
        mx = sb("mx", [P, 2, H])
        sm = sb("sm", [P, 2, H])
        ri = sb("ri", [P, 2, H])
        norm = [dict(st=sb(f"st{i}", [P, GP, 6]), mv=sb(f"mv{i}", [P, GP, 2]), ve=sb(f"ve{i}", [P, GP]),
                     rs=sb(f"rs{i}", [P, GP])) for i in range(3)]
        xp = sb("xp", [P, GP, D])
        zrow = sb("zrow", [P, GP, D + 2])
        z2T = sb("z2T", [P, TG])
        rt = sb("rt", [P, 10, GP, E])
        rq = sb("rq", [P, 9, GP])
        chosen_b = sb("chosen_b", [P, GP, E], BF16)
        next_slot = sb("next_slot", [P, E])
        slot_ix = sb("slot_ix", [P, 2, GP], I32)
        slot_ix_last = sb("slot_ix_last", [P, 2, GP], I32)
        wgt = sb("wgt", [P, 2, NP])
        group_step = sb("group_step", [P, GP])
        pad_rows = sb("pad_rows", [P, TILE // P, D + 2])
        idle = sb("idle", [P, 1])
        idle_p = sb("idle_p", [P, 1])

        wq_s = kf[:, 0:2, :]
        wk_s = kf[:, 2:4, :]
        wv_s = kf[:, 4:6, :]
        wo_s = kf[:, 6:8, :].rearrange("p a (j n) -> p (a j) n", n=D)
        wT = kf[:, 8:14, :].rearrange("p (w a) (j n) -> p w (a j) n", w=3, n=P)
        mask_raw = es.enter_context(nc.sbuf_tensor("mask_raw", [2, NP, S], U8))
        mask_row = vf[0][0:2, :, :, :].rearrange("p a j n -> p (a j n)").bitcast(BF16).rearrange(
            "p (n s) -> p n s", s=S)

        w1_raw = vf[1][:, :, :, :].rearrange("p a j n -> p (a j n)").rearrange("p (e f) -> p e f", f=HF)

        zlast = pr[0][:, :, :].rearrange("p h s -> p (h s)")[:, 0:GP * (D + 2)].rearrange("p (t c) -> p t c", t=GP)

        flat = kf[:, :, :].rearrange("p h t -> p (h t)")
        cursor = [0]

        def part(*shape):
            n = 1
            for d in shape:
                n *= d
            cols = flat[:, cursor[0]:cursor[0] + n]
            cursor[0] += n
            assert cursor[0] <= H * TG
            if len(shape) == 1:
                return cols
            names = "abc"[:len(shape)]
            return cols.rearrange(f"p ({' '.join(names)}) -> p {' '.join(names)}",
                                  **dict(zip(names[1:], shape[1:])))

        TJ = TILE // P
        tile_cmp, tile_cnt = part(NT, E), part(NT, E)
        tile_no, tile_e, tile_st, tile_row, tile_code, tile_live = (part(NT) for _ in range(6))
        reg_cmp = part(E, NB_MAX)
        tri, tri_n = part(E, E), part(E, E)
        n_tok, n_tile, tile_end = part(E), part(E), part(E)
        DEEP = 4
        zin = [part(TJ, D + 2) for _ in range(DEEP)]
        w_f = [part(B2 + D) for _ in range(DEEP)]
        y_sb = [part(TJ, D) for _ in range(DEEP)]
        ix_f = [part(2, TJ) for _ in range(DEEP)]
        y_in = [part(2, GP, D) for _ in range(2)] + [
            v[:, :, :, :].rearrange("p a j n -> p (a j n)")[:, 0:2 * GP * D].rearrange(
                "p (k t d) -> p k t d", k=2, t=GP) for v in vf]
        hid = [p[:, 8 * i:8 * i + 8, :].rearrange("p h s -> p (h s)").rearrange("p (c t) -> p c t", c=FC)
               for p in pr for i in range(2)]
        w_r = [Ah[:, 4 * i:4 * i + 4, :].rearrange("p h d -> p (h d)") for i in range(DEEP)]
        z_hi = [c[:, TILE * i:TILE * (i + 1)] for c in (cTh, cTl) for i in range(2)]
        z_lo = [Al[:, 2 * i:2 * i + 2, :].rearrange("p h d -> p (h d)") for i in range(DEEP)]
        tile_row_i = sb("tile_row_i", [P, NT], I32)
        tile_e_i = sb("tile_e_i", [P, NT], I32)
        next_i = sb("next_i", [P, E], I32)
        ix_i = [sb(f"ix_i{i}", [P, TJ], I32) for i in range(DEEP)]
        pad_ix = sb("pad_ix", [P, DEEP, TJ])
        k_tile = sb("k_tile", [P, NB_MAX])

        slots = nc.dram_tensor("slots", [REGION * E + TILE, D + 2], F32, kind="Internal").ap()
        mixed = nc.dram_tensor("mixed", [2 * B * S + DEEP * TILE, D], F32, kind="Internal").ap()

        bank = [es.enter_context(nc.psum_tensor(f"bank{i}", [P, 512], F32)) for i in range(8)]
        ring = bank[0:RING]
        s_ps = bank[4:6]
        t_ps = bank[6]
        o_ps = bank[7]

        ld_w = [sem(f"ld_w{i}") for i in range(4)]
        ld_m, ld_v, ld_e, ld_g, ld_b = (sem(n) for n in ("ld_m", "ld_v", "ld_e", "ld_g", "ld_b"))
        consts, pro_t, pro_tc, pro_m, pro_h, pro_l = (
            sem(n) for n in ("consts", "pro_t", "pro_tc", "pro_m", "pro_h", "pro_l"))
        mrow_ok, mk_ps, mk_ok, cq_ok, vec_ps, vec_ok, w1_ok = (
            sem(n) for n in ("mrow_ok", "mk_ps", "mk_ok", "cq_ok", "vec_ps", "vec_ok", "w1_ok"))
        unit = sem("unit")
        act_ev = sem("act_ev")
        dve_ev = sem("dve_ev")
        sc_ps = sem("sc_ps")
        sm_st = sem("sm_st")
        shifted = sem("shifted")
        exped = sem("exped")
        probs = sem("probs")
        t_full = sem("t_full")
        t_ev = sem("t_ev")
        att_ps = sem("att_ps")
        att_ok = sem("att_ok")
        st_ok = sem("st_ok")
        rs_ok = sem("rs_ok")
        z_ok = sem("z_ok")
        bo_ok = sem("bo_ok")
        zc_ok, xc_ok, nc_ok = (sem(n) for n in ("zc_ok", "xc_ok", "nc_ok"))
        s1_ok, r1_ok, xp_ok, s2_ok, r2_ok, zn_ok, base_ok = (
            sem(n) for n in ("s1_ok", "r1_ok", "xp_ok", "s2_ok", "r2_ok", "zn_ok", "base_ok"))
        rt_ok = sem("rt_ok")
        lg_ok = sem("lg_ok")
        ex_ok = sem("ex_ok")
        ch_ok = sem("ch_ok")
        ix_ok = sem("ix_ok")
        tok_ok = sem("tok_ok")
        sent = sem("sent")
        idle_ok = sem("idle_ok")
        fold_ps, fold_ok = sem("fold_ps"), sem("fold_ok")
        sl_ok = sem("sl_ok")
        tn_ok = sem("tn_ok")
        tab = sem("tab")
        pad_ok = sem("pad_ok")
        zi = [sem(f"zi{i}") for i in range(DEEP)]
        out_s = [sem(f"out_s{i}") for i in range(DEEP)]
        wc_ok = sem("wc_ok")
        ct_ps, ch_hi, cl_lo, up_ps, gl_ok, dn_ps, yv_ok, yi_ok, yi_st = (
            sem(n) for n in ("ct_ps", "ch_hi", "cl_lo", "up_ps", "gl_ok", "dn_ps", "yv_ok", "yi_ok", "yi_st"))
        yl = [sem(f"yl{i}") for i in range(4)]
        fin = sem("fin")
        stored = sem("stored")

        block = es.enter_context(nc.Block())

        ROUTE = 23

        def group_of(g, first=False):
            return Group(ORDER_FIRST, False, 0) if first else Group(ORDER, True, g - 1)

        start = Group(PREP, False, 0)
        TAIL_UNIT, TAIL_ACT, TAIL_DVE = (
            total(PREP + ORDER_FIRST, who) + total(ORDER, who) * (NG - 1) - total(PREP, who) for who in (None, 0, 1))

        @block.sync
        def _(sp):
            sp.dma_start(wq_s, Wq.rearrange("d (a n) -> d a n", a=2)).then_inc(ld_w[0], 16)
            sp.dma_start(wk_s, Wk.rearrange("d (a n) -> d a n", a=2)).then_inc(ld_w[1], 16)
            sp.dma_start(wv_s, Wv.rearrange("d (a n) -> d a n", a=2)).then_inc(ld_w[2], 16)
            sp.dma_start(wo_s, Wo.rearrange("(j p) n -> p j n", p=P)).then_inc(ld_w[3], 16)
            sp.dma_start(xs[:, 0:GP, :], x_t[:, 0:GP, :]).then_inc(ld_g, 16)
            sp.dma_start(c_in[:, :, :], c_t[:, 0:GP, :]).then_inc(ld_g, 16)
            sp.dma_start(w1_raw, W1.rearrange("e d f -> d e f")).then_inc(ld_e, 16)
            for e in range(E):
                sp.dma_start(experts[:, e, 2 * HF:2 * HF + FC * D].rearrange("p (c n) -> p c n", n=D),
                             W2[e].rearrange("(c p) n -> p c n", p=P)).then_inc(ld_e, 16)
            sp.wait_ge(consts, CONSTS)
            sp.dma_start(slots[E * REGION:E * REGION + TILE, :].rearrange("(j p) c -> p j c", p=P),
                         pad_rows[:, :, :]).then_inc(pad_ok, 16)
            sp.wait_ge(unit, start.done("CB"))
            sp.dma_start(xs[:, GP:2 * GP, :], x_t[:, GP:2 * GP, :]).then_inc(ld_g, 16)
            sp.dma_start(c_in[:, :, :], c_t[:, GP:2 * GP, :]).then_inc(ld_g, 16)
            sp.wait_ge(unit, group_of(0, True).done("CB"))
            sp.dma_start(xs[:, 2 * GP:3 * GP, :], x_t[:, 2 * GP:3 * GP, :]).then_inc(ld_g, 16)
            sp.dma_start(c_in[:, :, :], c_t[:, 2 * GP:3 * GP, :]).then_inc(ld_g, 16)
            with sp.Fori(3, NG) as g:
                sp.wait_ge(unit, group_of(g - 2).done("CB"))
                sp.dma_start(xs[:, bass.ds(g * GP, GP), :], x_t[:, bass.ds(g * GP, GP), :]).then_inc(ld_g, 16)
                sp.dma_start(c_in[:, :, :], c_t[:, bass.ds(g * GP, GP), :]).then_inc(ld_g, 16)

            sp.wait_ge(att_ps, 2 * NP)
            sp.dma_start(w1_raw, W1.rearrange("e d f -> d e f")).then_inc(ld_b, 16)
            sp.wait_ge(tab, TAB_NEXT)
            for e in range(E):
                row = sp.value_load(next_i[0:1, e:e + 1], min_val=0, max_val=REGION * E - TILE)
                sp.dma_start(slots[bass.ds(row, TILE), :].rearrange("(j p) c -> p j c", p=P),
                             pad_rows[:, :, :]).then_inc(pad_ok, 16)
            sp.wait_ge(pad_ok, 16 * (E + 1))
            sp.wait_ge(sent, 32 * GP * NG)
            sp.wait_ge(tab, TAB_ALL)

            def load_tile(s, buf):
                row = sp.value_load(tile_row_i[0:1, bass.ds(s, 1)], min_val=0, max_val=REGION * E)
                sp.dma_start(zin[buf], slots[bass.ds(row, TILE), :].rearrange("(j p) c -> p j c", p=P)).then_inc(
                    zi[buf], 16)

            for s in range(DEEP):
                load_tile(s, s)
            with sp.Fori(1, NT // DEEP) as ss:
                for buf in range(DEEP):
                    s = DEEP * ss + buf
                    sp.wait_ge(ct_ps, s - DEEP + 1)
                    sp.wait_ge(yi_st, 2 * (s - DEEP) + 2)
                    load_tile(s, buf)

            for buf in range(DEEP):
                sp.wait_ge(out_s[buf], 16 * TJ * (NT // DEEP))

            def load_y(g, buf):
                for k in range(2):
                    sp.dma_start(y_in[buf][:, k], mixed[bass.ds(k * NTOK + g * TG, TG), :].rearrange(
                        "(t p) d -> p t d", p=P)).then_inc(yl[buf], 16)

            for g in range(4):
                load_y(g, g)
            with sp.Fori(0, NG // 4 - 1) as gg:
                for buf in range(4):
                    g = 4 * gg + buf
                    sp.wait_ge(fin, 2 * GP * g + 2 * GP)
                    sp.dma_start(out_t[:, bass.ds(g * GP, GP), :], xs[:, bass.ds(g * GP, GP), :]).then_inc(stored, 16)
                    load_y(g + 4, buf)
            for g in range(NG - 4, NG):
                sp.wait_ge(fin, 2 * GP * g + 2 * GP)
                sp.dma_start(out_t[:, g * GP:g * GP + GP, :], xs[:, g * GP:g * GP + GP, :]).then_inc(stored, 16)
            sp.wait_ge(stored, 16 * NG)

        @block.gpsimd
        def _(pool):
            pool.memset(ident[:, :], 0.0).then_inc(consts, 1)
            pool.memset(ident_b[:, :], 0.0).then_inc(consts, 1)
            pool.memset(causal[:, :], 0.0).then_inc(consts, 1)
            pool.memset(sel2[:, :], 1.0).then_inc(consts, 1)
            pool.memset(half[:, :], -0.5).then_inc(consts, 1)
            pool.memset(upper_b[:, :], 1.0).then_inc(consts, 1)
            pool.memset(ones_b[:, :], 1.0).then_inc(consts, 1)
            pool.memset(ones_row[:, :], 1.0).then_inc(consts, 1)
            pool.memset(group_step[:, :], float(TG)).then_inc(consts, 1)
            pool.memset(pad_rows[:, :, :], 0.0).then_inc(consts, 1)
            for e in range(E):
                pool.memset(rank[:, e:e + 1], float(E - e)).then_inc(consts, 1)
                pool.memset(region[:, e:e + 1], float(REGION * e)).then_inc(consts, 1)
            pool.iota(zrow[:, :, D], pattern=[[P, GP]], base=0, channel_multiplier=1,
                      allow_small_or_imprecise_dtypes=True).then_inc(consts, 1)
            pool.iota(pad_ix[:, :, :], pattern=[[TILE, DEEP], [P, TILE // P]], base=2 * NTOK, channel_multiplier=1,
                      allow_small_or_imprecise_dtypes=True).then_inc(consts, 1)
            pool.iota(k_tile[:, :], pattern=[[TILE, NB_MAX]], base=0, channel_multiplier=0,
                      allow_small_or_imprecise_dtypes=True).then_inc(consts, 1)
            pool.wait_ge(consts, CONSTS - 7)
            pool.memset(pad_rows[:, :, D:D + 1], PAD_TOKEN).then_inc(consts, 1)
            pool.affine_select(out=upper_b[:, :], in_=upper_b[:, :], compare_op=ALU.is_gt, fill=0.0,
                               base=0, pattern=[[1, P]], channel_multiplier=-1).then_inc(consts, 1)
            pool.affine_select(out=ident[:, :], in_=ident[:, :], compare_op=ALU.not_equal, fill=1.0,
                               base=0, pattern=[[-1, P]], channel_multiplier=1).then_inc(consts, 1)
            pool.affine_select(out=ident_b[:, :], in_=ident_b[:, :], compare_op=ALU.not_equal, fill=1.0,
                               base=0, pattern=[[-1, P]], channel_multiplier=1).then_inc(consts, 1)
            pool.affine_select(out=causal[:, :], in_=causal[:, :], compare_op=ALU.is_ge, fill=NEG,
                               base=0, pattern=[[-1, P]], channel_multiplier=1).then_inc(consts, 1)
            pool.affine_select(out=sel2[:, :], in_=sel2[:, :], compare_op=ALU.is_ge, fill=0.0,
                               base=0, pattern=[[1, P]], channel_multiplier=-S).then_inc(consts, 1)
            pool.wait_ge(consts, CONSTS - 1)
            pool.affine_select(out=sel2[:, :], in_=sel2[:, :], compare_op=ALU.is_ge, fill=0.0,
                               base=S - 1, pattern=[[-1, P]], channel_multiplier=S).then_inc(consts, 1)

            def before_scatter():
                pool.tensor_tensor(idle_p[:, :], half[:, 0:1], half[:, 0:1], ALU.mult).then_inc(idle_ok, 1)

            def normalize(m, ready, n, src, dst, mid, dev, done):
                pool.wait_ge(ready, 9 * n + 9)
                pool.tensor_tensor(m["rs"][:, :], m["ve"][:, :], half[:, :], ALU.pow).then_inc(dev, 1)
                pool.tensor_tensor(dst, src, m["mv"][:, :, 0].unsqueeze(2).to_broadcast([P, GP, D]),
                                   ALU.subtract).then_inc(mid, 1)
                pool.wait_ge(mid, n + 1)
                pool.wait_ge(dev, n + 1)
                pool.tensor_tensor(dst, dst, m["rs"][:, :].unsqueeze(2).to_broadcast([P, GP, D]),
                                   ALU.mult).then_inc(done, GP)

            def prep(g, transposed=None):
                if transposed is not None:
                    pool.wait_ge(unit, transposed)
                normalize(norm[0], st_ok, g, xs[:, bass.ds(g * GP, GP), :], z[:, :, :], zc_ok, rs_ok, z_ok)
                pool.tensor_tensor(xs[:, bass.ds(g * GP, GP), :], xs[:, bass.ds(g * GP, GP), :],
                                   bo_b[:, :].unsqueeze(1).to_broadcast([P, GP, D]), ALU.add).then_inc(bo_ok, 1)

            def x1_norm(r, first=False):
                if not first:
                    pool.wait_ge(base_ok, r)
                    pool.wait_ge(s2_ok, 9 * r)
                normalize(norm[1], s1_ok, r, xs[:, bass.ds(r * GP, GP), :], xp[:, :, :], xc_ok, r1_ok, xp_ok)

            def z2_norm(r, rows=zrow, first=False):
                if not first:
                    pool.wait_ge(sent, 32 * GP * r)
                normalize(norm[2], s2_ok, r, xp[:, :, :], rows[:, :, 0:D], nc_ok, r2_ok, zn_ok)
                pool.tensor_tensor(xs[:, bass.ds(r * GP, GP), :], xs[:, bass.ds(r * GP, GP), :], xp[:, :, :],
                                   ALU.add).then_inc(base_ok, 1)

            def next_tokens(r):
                pool.wait_ge(sent, 32 * GP * r)
                pool.tensor_tensor(zrow[:, :, D], zrow[:, :, D], group_step[:, :], ALU.add).then_inc(tok_ok, 1)
                pool.wait_ge(tok_ok, r)

            def send(r, rows=zrow, ix=slot_ix):
                if not (isinstance(r, int) and r == 0):
                    pool.wait_ge(idle_ok, r)
                pool.wait_ge(zn_ok, GP * r + GP)
                pool.wait_ge(ix_ok, r + 1)
                before_scatter()
                for k in range(2):
                    for t in range(GP):
                        pool.indirect_dma_start(
                            out=slots, out_offset=bass.IndirectOffsetOnAxis(ap=ix[:, k, t:t + 1], axis=0),
                            in_=rows[:, t, :], in_offset=None).then_inc(sent, 16)

            pool.wait_ge(ld_v, 16 * 7)
            prep(0)
            prep(1, start.done("ZB"))
            x1_norm(0, first=True)
            z2_norm(0, first=True)
            prep(2, group_of(0, True).done("ZB"))
            send(0)
            with pool.Fori(2, NG - 1) as g:
                x1_norm(g - 1)
                z2_norm(g - 1)
                prep(g + 1, group_of(g - 1).done("ZB"))
                next_tokens(g - 1)
                send(g - 1)
            x1_norm(NG - 2)
            z2_norm(NG - 2)
            next_tokens(NG - 2)
            send(NG - 2)
            pool.wait_ge(t_full, 2 * NP - 2)
            pool.iota(zlast[:, :, D], pattern=[[P, GP]], base=TG * (NG - 1), channel_multiplier=1,
                      allow_small_or_imprecise_dtypes=True).then_inc(tok_ok, 1)
            x1_norm(NG - 1)
            z2_norm(NG - 1, zlast, first=True)
            pool.wait_ge(att_ps, 2 * NP)
            pool.iota(tile_no, pattern=[[1, NT]], base=0, channel_multiplier=0,
                      allow_small_or_imprecise_dtypes=True).then_inc(tn_ok, 1)
            pool.wait_ge(tok_ok, NG - 1)
            send(NG - 1, zlast, slot_ix_last)

            with pool.Fori(0, NT // DEEP) as ss:
                for buf in range(DEEP):
                    s = DEEP * ss + buf
                    pool.wait_ge(idle_ok, NG + s)
                    pool.wait_ge(yv_ok, s + 1)
                    pool.wait_ge(yi_ok, s + 1)
                    before_scatter()
                    for j in range(TJ):
                        pool.indirect_dma_start(
                            out=mixed, out_offset=bass.IndirectOffsetOnAxis(ap=ix_i[buf][:, j:j + 1], axis=0),
                            in_=y_sb[buf][:, j, :], in_offset=None).then_inc(out_s[buf], 16)

        @block.scalar
        def _(act):
            act.dma_start(mask_raw[:, :, :], mask.rearrange("(n two) s -> two n s", two=2)).then_inc(ld_m, 16)
            act.dma_start(vec_rows[0:E * FC, :], b1.rearrange("e (c p) -> (e c) p", p=P)).then_inc(ld_v, 16)
            act.dma_start(vec_rows[E * FC:E * FC + 1, :], ln_g.rearrange("(a d) -> a d", a=1)).then_inc(ld_v, 16)
            act.dma_start(vec_rows[E * FC + 1:E * FC + 2, :], ln_b.rearrange("(a d) -> a d", a=1)).then_inc(ld_v, 16)
            act.dma_start(bo_b[:, :], bo.rearrange("(a d) -> a d", a=1).to_broadcast([P, D])).then_inc(ld_v, 16)
            act.dma_start(rb_b[:, :], rb.rearrange("(a d) -> a d", a=1).to_broadcast([P, E])).then_inc(ld_v, 16)
            act.dma_start(rW_s[:, :], rW).then_inc(ld_v, 16)
            act.dma_start(experts[:, :, 2 * HF + B2:], b2.rearrange("(a e) d -> a e d", a=1).to_broadcast([P, E, D])).then_inc(ld_v, 16)

            def prep_units(gr):
                for k, name in enumerate(PREP):
                    act.wait_ge(unit, gr.done(name))
                    dst = zT if k < 2 else cTh
                    act.activation(dst[:, 256 * (k % 2):256 * (k % 2) + 256], ring[gr.bank(name)][:, 0:256],
                                   ACT.Copy).then_inc(act_ev, 1)

            for k in range(3):
                act.wait_ge(pro_t, k + 1)
                act.activation(wT[:, k // 2, 4 * (k % 2):4 * (k % 2) + 4, :],
                               bank[k].rearrange("p (j n) -> p j n", n=P), ACT.Copy).then_inc(pro_tc, 1)
            Ap = Ah[:, :, :].rearrange("p (q two) d -> p two q d", two=2)
            for k in range(8):
                act.wait_ge(pro_m, k + 1)
                src = bank[k].rearrange("p (j n) -> p j n", n=D)
                if k < 4:
                    act.activation(Ap[:, k // 2, 4 * (k % 2):4 * (k % 2) + 4, :], src, ACT.Copy,
                                   scale=DH ** -0.5).then_inc(pro_h, 1)
                else:
                    act.activation(Nh[:, (k - 4) // 2, 4 * (k % 2):4 * (k % 2) + 4, :], src,
                                   ACT.Copy).then_inc(pro_h, 1)

            def r_units(done, banks):
                for k in range(2):
                    act.wait_ge(unit, done[k])
                    act.activation(z2T[:, 256 * k:256 * k + 256], ring[banks[k]][:, 0:256],
                                   ACT.Copy).then_inc(act_ev, 1)

            def r_exp(r):
                act.wait_ge(lg_ok, r + 1)
                act.activation(rt[:, 1], rt[:, 0], ACT.Exp).then_inc(ex_ok, 1)

            def t_unit(n, par, t):
                act.wait_ge(t_full, 2 * n + t + 1)
                if not (isinstance(n, int) and n == 0):
                    act.wait_ge(att_ps, 2 * n + t - 1)
                act.activation(pT[:, 4 * t:4 * t + 4, :], t_ps.rearrange("p (j n) -> p j n", n=P),
                               ACT.Copy).then_inc(t_ev, 1)

            def exp_half(n, par, t):
                act.wait_ge(shifted, 2 * n + t + 1)
                act.activation(pr[par][:, 8 * t:8 * t + 8, :], pr[par][:, 8 * t:8 * t + 8, :],
                               ACT.Exp).then_inc(exped, 1)

            def group(g, first=False, last=False):
                gr, r = group_of(g, first), g - 1
                for h, name in enumerate(KEYS):
                    if unit_owner(name)[0]:
                        act.wait_ge(unit, gr.done(name))
                        act.activation(kf[:, h, :], ring[gr.bank(name)][:, :], ACT.Copy).then_inc(act_ev, 1)
                    if not first and h in (1, 4):
                        t_unit(GP * g - 1, 1, (h - 1) // 3)
                for i in range(GP):
                    n, par = GP * g + i, i % 2
                    for k, name in enumerate(values(i)):
                        act.wait_ge(unit, gr.done(name))
                        if k == 0 and not (first and i < 2):
                            act.wait_ge(att_ps, 2 * n - 2)
                        if first and k == 0 and i < 2:
                            act.wait_ge(w1_ok, 5)
                            act.wait_ge(mk_ps, 8)
                        par_h, q4 = k // 2, k % 2
                        for b in range(2):
                            act.activation(vf[par][64 * par_h:64 * par_h + 64, b, 4 * q4:4 * q4 + 4, :],
                                           ring[gr.bank(name)][64 * b:64 * b + 64, :].rearrange(
                                               "p (j n) -> p j n", n=D), ACT.Copy).then_inc(act_ev, 1)
                        if k == 0:
                            if i > 0:
                                t_unit(n - 1, 1 - par, 0)
                            exp_half(n, par, 0)
                            if not first and i == 1:
                                r_units([gr.done("RA"), gr.done("RB")], [gr.bank("RA"), gr.bank("RB")])
                        if k == 1:
                            exp_half(n, par, 1)
                            if i > 0:
                                t_unit(n - 1, 1 - par, 1)
                    if not first and i == 2:
                        r_exp(r)
                if not last:
                    prep_units(gr)

            prep_units(start)
            group(0, first=True)
            group(1)
            with act.Fori(2, NG - 1) as g:
                group(g)
            group(NG - 1, last=True)
            for t in range(2):
                t_unit(NP - 1, 1, t)
            r_units([TAIL_UNIT + 1, TAIL_UNIT + 2], [0, 1])
            r_exp(NG - 1)

            def hi_part(s, deep):
                act.wait_ge(ct_ps, s + 1)
                if not isinstance(s, int) or s >= DEEP:
                    act.wait_ge(up_ps, s - DEEP + 1)
                act.activation(z_hi[deep], bank[deep % 2][:, 0:TILE], ACT.Copy).then_inc(ch_hi, 1)

            def hidden(s, deep):
                act.wait_ge(up_ps, s + 1)
                if not isinstance(s, int) or s >= DEEP:
                    act.wait_ge(dn_ps, s - DEEP + 1)
                for c in range(FC):
                    act.activation(hid[deep][:, c, :], bank[2 + deep % 2][:, c * TILE:(c + 1) * TILE], ACT.Gelu,
                                   bias=w_f[deep][:, B1 + c:B1 + c + 1]).then_inc(gl_ok, 1)

            def results(s, deep):
                act.wait_ge(dn_ps, s + 1)
                if not isinstance(s, int) or s >= DEEP:
                    act.wait_ge(out_s[deep], 4 * TJ * (s - deep))
                act.activation(y_sb[deep], bank[4 + deep % 2][:, 0:TJ * D].rearrange("p (j d) -> p j d", d=D),
                               ACT.Copy).then_inc(yv_ok, 1)

            for s in range(2 * DEEP):
                hi_part(s, s % DEEP)
                if s >= 3:
                    results(s - 3, (s - 3) % DEEP)
                if s >= 1:
                    hidden(s - 1, (s - 1) % DEEP)
            with act.Fori(1, NT // (2 * DEEP)) as ss:
                for k in range(2 * DEEP):
                    hi_part(2 * DEEP * ss + k, k % DEEP)
                    results(2 * DEEP * ss + k - 3, (k - 3) % DEEP)
                    hidden(2 * DEEP * ss + k - 1, (k - 1) % DEEP)
            results(NT - 3, DEEP - 3)
            hidden(NT - 1, DEEP - 1)
            results(NT - 2, DEEP - 2)
            results(NT - 1, DEEP - 1)

        @block.tensor
        def _(pe):
            def split_product(ps, lh, ll, rh, rl):
                pe.matmul(ps, lh, rh, start=True, stop=False)
                pe.matmul(ps, lh, rl, start=False, stop=False)
                return pe.matmul(ps, ll, rh, start=False, stop=True)

            pe.wait_ge(consts, CONSTS)
            for k in range(6):
                w = (wq_s, wk_s, wv_s)[k // 2]
                pe.wait_ge(ld_w[k // 2], 16)
                for j in range(4):
                    last = pe.transpose(bank[k][:, j * P:(j + 1) * P], w[:, k % 2, j * P:(j + 1) * P], ident[:, :])
                last.then_inc(pro_t, 1)
            pe.wait_ge(pro_tc, 6)
            pe.wait_ge(ld_w[3], 16)
            for k in range(8):
                hp, q4 = (k // 2) % 2, k % 2
                rows = slice(64 * hp, 64 * hp + 64)
                if k == 4:
                    pe.wait_ge(ld_v, 16 * 7)
                    pe.transpose(bank[7][:, 0:E * FC + 2], vec_rows[:, :],
                                 ident[0:E * FC + 2, 0:E * FC + 2]).then_inc(vec_ps, 1)
                if k == 7:
                    pe.wait_ge(vec_ok, 1)
                for q in range(4):
                    j = 4 * q4 + q
                    lhs = wT[rows, 1, j, :] if k < 4 else wT[rows, 2, j, :]
                    rhs = wT[rows, 0, j, :] if k < 4 else wo_s[rows, j, :]
                    last = pe.matmul(bank[k][:, q * D:(q + 1) * D], lhs, rhs, start=True, stop=True)
                last.then_inc(pro_m, 1)
            pe.wait_ge(mrow_ok, 2)
            for k in range(8):
                pe.wait_ge(pro_l, k + 1)
                pe.matmul(bank[k][:, :].rearrange("p (n s) -> p n s", s=S), sel2[:, :],
                          mask_row[:, 8 * k:8 * k + 8, :], start=True, stop=True).then_inc(mk_ps, 1)

            def ring_free(gr, name):
                who, value = gr.freed(name)
                pe.wait_ge(dve_ev if who else act_ev, value)

            def prep_units(gr, g, names, free=True):
                for name in names:
                    k = PREP.index(name)
                    if free:
                        ring_free(gr, name)
                    if k == 0:
                        pe.wait_ge(z_ok, GP * g + GP)
                    if k == 2:
                        pe.wait_ge(ld_g, 32 * g + 32)
                    for t in range(2):
                        tile = 2 * (k % 2) + t
                        src = z[:, tile, :] if k < 2 else c_in[:, tile, :]
                        last = pe.transpose(ring[gr.bank(name)][:, t * P:(t + 1) * P], src, ident[:, :])
                    last.then_inc(unit, 1)

            def r_transposes(r, k, ps, rows=zrow):
                pe.wait_ge(zn_ok, GP * r + GP)
                for t in range(2):
                    last = pe.transpose(ps[:, t * P:(t + 1) * P], rows[:, 2 * k + t, 0:D], ident[:, :])
                last.then_inc(unit, 1)

            def r_logits(ps):
                for t in range(GP):
                    last = pe.matmul(ps[:, t * E:(t + 1) * E], z2T[:, t * P:(t + 1) * P], rW_g[:, :],
                                     start=True, stop=True)
                last.then_inc(unit, 1)

            def r_ranks(r, ps):
                pe.wait_ge(ch_ok, r + 1)
                pe.matmul(ps[:, 0:GP * E].rearrange("p (t e) -> p t e", e=E), upper_b[:, :], chosen_b[:, :, :],
                          start=True, stop=False, skip_group_check=True)
                for t in range(GP - 1):
                    later = GP - 1 - t
                    pe.matmul(ps[:, (t + 1) * E:GP * E].rearrange("p (t e) -> p t e", e=E), ones_b[:, :],
                              chosen_b[:, t, :].unsqueeze(1).to_broadcast([P, later, E]),
                              start=False, stop=(t == GP - 2), skip_group_check=True)
                for t in range(GP):
                    last = pe.matmul(ps[:, GP * E:GP * E + E], ones_b[:, :], chosen_b[:, t, :],
                                     start=(t == 0), stop=(t == GP - 1), skip_group_check=True)
                last.then_inc(unit, 1)

            def t_half(n, par, t):
                pe.wait_ge(probs, 2 * n + t + 1)
                if t == 1 or not (isinstance(n, int) and n == 0):
                    pe.wait_ge(t_ev, 2 * n + t)
                for q in range(4):
                    j = 4 * t + q
                    last = pe.transpose(t_ps[:, q * P:(q + 1) * P],
                                        pr[par][:, 2 * j:2 * j + 2, :].rearrange("p a s -> p (a s)"), ident[:, :])
                last.then_inc(t_full, 1)

            def attend(n, par, t):
                pe.wait_ge(t_ev, 2 * n + t + 1)
                if t == 0 and not (isinstance(n, int) and n == 0):
                    pe.wait_ge(att_ok, n)
                for j in range(4 * t, 4 * t + 4):
                    for b in range(2):
                        last = pe.matmul(o_ps[64 * b:64 * b + 64, 0:D], pT[:, j, 64 * b:64 * b + 64],
                                         vf[par][:, b, j, :], start=(j == 0), stop=(j == H // 2 - 1),
                                         skip_group_check=True)
                last.then_inc(att_ps, 1)

            def scores(g, i, hf):
                n = GP * g + i
                if not (isinstance(n, int) and n == 0):
                    pe.wait_ge(shifted, 2 * n + hf - 1)
                heads = s_ps[hf][:, :].rearrange("p (h s) -> p h s", s=S)
                mrow = mask_b[:, n, :].unsqueeze(1).to_broadcast([P, 8, S])
                pe.matmul(heads, ident_b[:, :], mrow, start=True, stop=False, skip_group_check=True)
                for b in range(2):
                    cols = slice(i * P + 64 * b, i * P + 64 * b + 64)
                    last = pe.matmul(heads[64 * b:64 * b + 64], zT[:, cols], kf[:, 8 * hf:8 * hf + 8, cols],
                                     start=False, stop=True, skip_group_check=True)
                last.then_inc(sc_ps, 1)

            def value_unit(gr, i, k):
                name = values(i)[k]
                ring_free(gr, name)
                toks = slice(i * P, (i + 1) * P)
                heads = (slice(None), k // 2, slice(4 * (k % 2), 4 * (k % 2) + 4), slice(None))
                split_product(ring[gr.bank(name)][:, :].rearrange("p (j n) -> p j n", n=D),
                              cTh[:, toks], cTl[:, toks], Nh[heads], Nl[heads]).then_inc(unit, 1)

            def group(g, first=False, last=False):
                gr, r = group_of(g, first), g - 1
                pe.wait_ge(dve_ev, gr._count(1, 0))
                for h, name in enumerate(KEYS):
                    ring_free(gr, name)
                    split_product(ring[gr.bank(name)][:, :], Ah[:, h, :], Al[:, h, :],
                                  cTh[:, :], cTl[:, :]).then_inc(unit, 1)
                    if not first:
                        if h == 1:
                            t_half(GP * g - 1, 1, 0)
                        if h == 4:
                            attend(GP * g - 1, 1, 0)
                            t_half(GP * g - 1, 1, 1)
                        if h == 7:
                            attend(GP * g - 1, 1, 1)
                for i in range(GP):
                    n, par = GP * g + i, i % 2
                    if first and i == 0:
                        pe.wait_ge(fold_ok, 1)
                    if i == 0:
                        pe.wait_ge(act_ev, gr.done("K7", 0))
                        pe.wait_ge(dve_ev, gr.done("K7", 1))
                    if i == 3:
                        value_unit(gr, i, 0)
                    scores(g, i, 0)
                    if i < 3:
                        value_unit(gr, i, 0)
                    if i == 0:
                        pe.wait_ge(act_ev, gr.done("K15", 0))
                        pe.wait_ge(dve_ev, gr.done("K15", 1))
                    scores(g, i, 1)
                    if i == 0:
                        for k in range(1, 4):
                            value_unit(gr, i, k)
                        continue
                    t_half(n - 1, 1 - par, 0)
                    if i == 1 and not first:
                        for k, name in enumerate(("RA", "RB")):
                            ring_free(gr, name)
                            r_transposes(r, k, ring[gr.bank(name)])
                    value_unit(gr, i, 1)
                    pe.wait_ge(act_ev, gr.done(values(i - 1)[3], 0))
                    if i < GP - 1:
                        attend(n - 1, 1 - par, 0)
                        t_half(n - 1, 1 - par, 1)
                        if i == 1 and not first:
                            ring_free(gr, "RL")
                            pe.wait_ge(act_ev, gr.done("RB", 0))
                            r_logits(ring[gr.bank("RL")])
                        if i == 2 and not first:
                            ring_free(gr, "RX")
                            r_ranks(r, ring[gr.bank("RX")])
                        value_unit(gr, i, 2)
                        attend(n - 1, 1 - par, 1)
                        value_unit(gr, i, 3)
                    else:
                        t_half(n - 1, 1 - par, 1)
                        value_unit(gr, i, 2)
                        attend(n - 1, 1 - par, 0)
                        value_unit(gr, i, 3)
                        if not last:
                            prep_units(gr, g + 1, PREP)
                        attend(n - 1, 1 - par, 1)

            pe.wait_ge(mk_ok, 4)
            prep_units(start, 0, PREP, free=False)
            pe.wait_ge(mk_ok, 8)
            pe.wait_ge(vec_ok, 2)
            pe.matmul(bank[6][:, 0:E], bc_wide[:, :], rW_s[:, :], start=True, stop=True).then_inc(fold_ps, 1)
            group(0, first=True)
            group(1)
            with pe.Fori(2, NG - 1) as g:
                group(g)
            group(NG - 1, last=True)
            for t in range(2):
                t_half(NP - 1, 1, t)
            pe.wait_ge(act_ev, TAIL_ACT)
            attend(NP - 1, 1, 0)
            attend(NP - 1, 1, 1)
            pe.wait_ge(dve_ev, TAIL_DVE)
            for k in range(2):
                r_transposes(NG - 1, k, ring[k], zlast)
            pe.wait_ge(act_ev, TAIL_ACT + 2)
            r_logits(ring[2])
            r_ranks(NG - 1, ring[3])
            pe.wait_ge(ld_b, 16)
            for u in range(E * FC):
                last = pe.matmul(bank[6][:, u:u + 1], w1_raw[:, u // FC, (u % FC) * P:(u % FC + 1) * P], bc,
                                 start=True, stop=True)
            last.then_inc(fold_ps, 1)

            def rows_t(s, deep):
                pe.wait_ge(zi[deep], 4 * (s - deep) + 16)
                if not isinstance(s, int) or s >= 2:
                    pe.wait_ge(cl_lo, s - 1)
                for j in range(TJ):
                    last = pe.transpose(bank[deep % 2][:, j * P:(j + 1) * P], zin[deep][:, j, 0:D], ident[:, :])
                last.then_inc(ct_ps, 1)

            def up(s, deep):
                pe.wait_ge(cl_lo, s + 1)
                pe.wait_ge(wc_ok, 2 * s + 2)
                if not isinstance(s, int) or s >= 2:
                    pe.wait_ge(gl_ok, FC * (s - 1))
                for c in range(FC):
                    last = split_product(bank[2 + deep % 2][:, c * TILE:(c + 1) * TILE],
                                         w_r[deep][:, c * P:(c + 1) * P], w_r[deep][:, HF + c * P:HF + (c + 1) * P],
                                         z_hi[deep], z_lo[deep])
                last.then_inc(up_ps, 1)

            def down(s, deep):
                pe.wait_ge(gl_ok, FC * (s + 1))
                if not isinstance(s, int) or s >= 2:
                    pe.wait_ge(yv_ok, s - 1)
                for j in range(TJ):
                    for c in range(FC):
                        pe.matmul(bank[4 + deep % 2][:, j * D:(j + 1) * D],
                                  hid[deep][:, c, j * P:(j + 1) * P], w_f[deep][:, c * D:(c + 1) * D],
                                  start=(c == 0), stop=False)
                    last = pe.matmul(bank[4 + deep % 2][:, j * D:(j + 1) * D], ones_row[:, :], w_f[deep][0:1, B2:],
                                     start=False, stop=True)
                last.then_inc(dn_ps, 1)

            rows_t(0, 0)
            rows_t(1, 1)
            up(0, 0)
            for s in range(2, DEEP):
                rows_t(s, s)
                up(s - 1, s - 1)
                down(s - 2, s - 2)
            with pe.Fori(1, NT // DEEP) as ss:
                for k in range(DEEP):
                    rows_t(DEEP * ss + k, k)
                    up(DEEP * ss + k - 1, (k - 1) % DEEP)
                    down(DEEP * ss + k - 2, (k - 2) % DEEP)
            up(NT - 1, DEEP - 1)
            down(NT - 2, DEEP - 2)
            down(NT - 1, DEEP - 1)

        @block.vector
        def _(dve):
            def norm_stats(src, m, done, g):
                for t in range(GP):
                    dve.bn_stats(m["st"][:, t, :], src(t)).then_inc(done, 1)
                dve.wait_ge(done, 9 * g + 4)
                dve.memset(idle[:, :], 0.0)
                for t in range(GP):
                    dve.bn_aggr(m["mv"][:, t, :], m["st"][:, t, :]).then_inc(done, 1)
                dve.wait_ge(done, 9 * g + 8)
                dve.tensor_scalar(m["ve"][:, :], m["mv"][:, :, 1], LN_EPS, None, ALU.add).then_inc(done, 1)

            def prep_stats(g):
                dve.wait_ge(ld_g, 32 * g + 32)
                norm_stats(lambda t: xs[:, g * GP + t, :], norm[0], st_ok, g)

            for k in range(3, 6):
                dve.wait_ge(pro_t, k + 1)
                dve.tensor_copy(wT[:, k // 2, 4 * (k % 2):4 * (k % 2) + 4, :],
                                bank[k].rearrange("p (j n) -> p j n", n=P)).then_inc(pro_tc, 1)
            def split_w1(k):
                if k == 0:
                    dve.wait_ge(ld_e, 16 * (E + 1))
                    dve.tensor_scalar(w1_raw, w1_raw, gc, None, ALU.mult).then_inc(w1_ok, 1)
                elif k == 1:
                    dve.wait_ge(w1_ok, 3)
                    dve.tensor_copy(experts[:, :, 0:HF].bitcast(F32R), w1_raw).then_inc(w1_ok, 1)
                else:
                    dve.wait_ge(w1_ok, 4)
                    dve.tensor_tensor(experts[:, :, HF:2 * HF].bitcast(F32R), w1_raw, experts[:, :, 0:HF],
                                      ALU.subtract).then_inc(w1_ok, 1)

            prep_stats(0)

            dve.wait_ge(ld_m, 16)
            for k in range(2):
                dve.tensor_scalar(mask_row[:, 32 * k:32 * k + 32, :], mask_raw[:, 32 * k:32 * k + 32, :], NEG, None,
                                  ALU.mult).then_inc(mrow_ok, 1)
            dve.wait_ge(consts, CONSTS)
            for b in range(2):
                dve.tensor_copy(causal_q[64 * b:64 * b + 64, :],
                                causal[64 * b:64 * b + 64, 64 * b:64 * b + 64]).then_inc(cq_ok, 1)
            Ahp = Ah[:, :, :].rearrange("p (q two) d -> p two q d", two=2)
            Alp = Al[:, :, :].rearrange("p (q two) d -> p two q d", two=2)
            for k in range(8):
                dve.wait_ge(pro_h, k + 1)
                src = bank[k].rearrange("p (j n) -> p j n", n=D)
                js = slice(4 * (k % 2), 4 * (k % 2) + 4)
                if k < 4:
                    dve.scalar_tensor_tensor(out=Alp[:, k // 2, js, :], in0=src, scalar=DH ** -0.5,
                                             in1=Ahp[:, k // 2, js, :].bitcast(F32), op0=ALU.mult,
                                             op1=ALU.subtract).then_inc(pro_l, 1)
                else:
                    dve.tensor_tensor(Nl[:, (k - 4) // 2, js, :], src, Nh[:, (k - 4) // 2, js, :].bitcast(F32),
                                      ALU.subtract).then_inc(pro_l, 1)
                if k == 3:
                    dve.wait_ge(vec_ps, 1)
                    dve.tensor_copy(vec_cols[:, :], bank[7][:, 0:E * FC + 2]).then_inc(vec_ok, 1)
                    dve.wait_ge(vec_ok, 1)
                    dve.tensor_copy(bc_wide[:, :], bc.to_broadcast([P, P])).then_inc(vec_ok, 1)
            dve.wait_ge(cq_ok, 2)
            for k in range(8):
                dve.wait_ge(mk_ps, k + 1)
                dve.tensor_tensor(mask_b[:, 8 * k:8 * k + 8, :], bank[k].rearrange("p (n s) -> p n s", s=S),
                                  causal_q[:, :].unsqueeze(1).to_broadcast([P, 8, S]), ALU.min).then_inc(mk_ok, 1)

            def prep_units(gr):
                for k, name in enumerate(("CA", "CB")):
                    dve.wait_ge(act_ev, gr.done(name, 0))
                    dve.tensor_tensor(cTl[:, 256 * k:256 * k + 256], ring[gr.bank(name)][:, 0:256],
                                      cTh[:, 256 * k:256 * k + 256].bitcast(F32), ALU.subtract).then_inc(dve_ev, 1)

            def add_attention(n):
                dve.wait_ge(att_ps, 2 * n + 2)
                dve.tensor_tensor(xs[:, n, :], o_ps[:, 0:D], xs[:, n, :], ALU.add).then_inc(att_ok, 1)

            def shift_half(n, par, t):
                hs = slice(8 * t, 8 * t + 8)
                src = s_ps[t][:, :].rearrange("p (h s) -> p h s", s=S)
                dve.wait_ge(sc_ps, 2 * n + t + 1)
                dve.reduce_max(mx[:, par, hs], src, AX_X).then_inc(sm_st, 1)
                dve.wait_ge(sm_st, 6 * n + t + 1)
                dve.tensor_tensor(pr[par][:, hs, :], src, mx[:, par, hs].unsqueeze(2).to_broadcast([P, 8, S]),
                                  ALU.subtract).then_inc(shifted, 1)

            def normalize_half(n, par, t):
                hs = slice(8 * t, 8 * t + 8)
                dve.wait_ge(exped, 2 * n + t + 1)
                dve.reduce_sum(sm[:, par, hs], pr[par][:, hs, :], AX_X).then_inc(sm_st, 1)
                dve.wait_ge(sm_st, 6 * n + 2 * t + 3)
                dve.reciprocal(ri[:, par, hs], sm[:, par, hs]).then_inc(sm_st, 1)
                dve.wait_ge(sm_st, 6 * n + 2 * t + 4)
                dve.tensor_tensor(pr[par][:, hs, :], pr[par][:, hs, :],
                                  ri[:, par, hs].unsqueeze(2).to_broadcast([P, 8, S]), ALU.mult).then_inc(probs, 1)

            wide_ranks = rank[:, :].unsqueeze(1).to_broadcast([P, GP, E])

            def wide(a):
                return a.unsqueeze(2).to_broadcast([P, GP, E])

            class Chain:

                def __init__(self, r, at):
                    self.r, self.at = r, at

                def step(self, ins):
                    self.at += 1
                    ins.then_inc(rt_ok, 1)
                    dve.wait_ge(rt_ok, ROUTE * self.r + self.at)

            def route_a(r, ps, ready, freed, rows=zrow, first=False):
                ch = Chain(r, 0)
                dve.wait_ge(unit, ready)
                dve.tensor_tensor(rt[:, 2], ps[:, 0:GP * E].rearrange("p (t e) -> p t e", e=E),
                                  rb_sum[:, :].unsqueeze(1).to_broadcast([P, GP, E]), ALU.add).then_inc(dve_ev, 1)
                dve.wait_ge(dve_ev, freed)
                ch.step(dve.reduce_max(rq[:, 0], rt[:, 2], AX_X))
                dve.tensor_tensor(rt[:, 0], rt[:, 2], wide(rq[:, 0]), ALU.subtract).then_inc(lg_ok, 1)
                dve.wait_ge(lg_ok, r + 1)
                ch.step(dve.scalar_tensor_tensor(out=rt[:, 3], in0=rt[:, 0], scalar=0.0, in1=wide_ranks,
                                                 op0=ALU.is_equal, op1=ALU.mult))
                if not first:
                    dve.wait_ge(sent, 32 * GP * r)
                ch.step(dve.reduce_max(rows[:, :, D + 1], rt[:, 3], AX_X))
                ch.step(dve.tensor_tensor(rt[:, 4], wide_ranks, wide(rows[:, :, D + 1]), ALU.is_equal))
                ch.step(dve.scalar_tensor_tensor(out=rt[:, 5], in0=rt[:, 4], scalar=-1e30, in1=rt[:, 0],
                                                 op0=ALU.mult, op1=ALU.add))
                ch.step(dve.reduce_max(rq[:, 2], rt[:, 5], AX_X))
                ch.step(dve.tensor_tensor(rt[:, 6], rt[:, 5], wide(rq[:, 2]), ALU.is_equal))
                ch.step(dve.tensor_tensor(rt[:, 6], rt[:, 6], wide_ranks, ALU.mult))
                ch.step(dve.reduce_max(rq[:, 3], rt[:, 6], AX_X))
                ch.step(dve.tensor_tensor(rt[:, 5], wide_ranks, wide(rq[:, 3]), ALU.is_equal))
                dve.tensor_tensor(chosen_b[:, :, :], rt[:, 4], rt[:, 5], ALU.add).then_inc(ch_ok, 1)
                assert ch.at == 10

            def route_b(r):
                ch = Chain(r, 13)
                dve.wait_ge(ex_ok, r + 1)
                dve.wait_ge(ix_ok, r + 1)
                ch.step(dve.reduce_sum(rq[:, 4], rt[:, 1], AX_X))
                ch.step(dve.tensor_tensor(rt[:, 7], rt[:, 1], chosen_b[:, :, :], ALU.mult))
                ch.step(dve.reduce_sum(rq[:, 5], rt[:, 7], AX_X))
                ch.step(dve.scalar_tensor_tensor(out=rq[:, 6], in0=rq[:, 4], scalar=1e-8, in1=rq[:, 5],
                                                 op0=ALU.mult, op1=ALU.max))
                ch.step(dve.reciprocal(rq[:, 7], rq[:, 6]))
                ch.step(dve.tensor_tensor(rt[:, 7], rt[:, 7], wide(rq[:, 7]), ALU.mult))
                for k in range(2):
                    dve.tensor_tensor(rt[:, 8 if k else 6], rt[:, 7], rt[:, 4 + k], ALU.mult).then_inc(rt_ok, 1)
                ch.at += 2
                dve.wait_ge(rt_ok, ROUTE * r + ch.at)
                for k in range(2):
                    ins = dve.reduce_sum(wgt[:, k, bass.ds(r * GP, GP)], rt[:, 8 if k else 6], AX_X)
                    ins.then_inc(rt_ok, 1)
                ch.at += 2
                assert ch.at == ROUTE

            def route_c(r, ps, ready, ix=slot_ix):
                ch = Chain(r, 10)
                dve.wait_ge(unit, ready)
                ch.step(dve.tensor_tensor(rt[:, 2], ps[:, 0:GP * E].rearrange("p (t e) -> p t e", e=E),
                                          next_slot[:, :].unsqueeze(1).to_broadcast([P, GP, E]), ALU.add))
                dve.tensor_tensor(next_slot[:, :], ps[:, GP * E:GP * E + E], next_slot[:, :],
                                  ALU.add).then_inc(dve_ev, 1)
                for k in range(2):
                    dve.tensor_tensor(rt[:, 8 + k], rt[:, 2], rt[:, 4 + k], ALU.mult).then_inc(rt_ok, 1)
                ch.at += 2
                dve.wait_ge(rt_ok, ROUTE * r + ch.at)
                for k in range(2):
                    dve.reduce_sum(rq[:, 4 + k], rt[:, 8 + k], AX_X).then_inc(sl_ok, 1)
                dve.wait_ge(sl_ok, 2 * r + 2)
                dve.tensor_copy(ix[:, :, :], rq[:, 4:6]).then_inc(ix_ok, 1)
                assert ch.at == 13

            def group(g, first=False, last=False):
                gr, r = group_of(g, first), g - 1
                if not first:
                    add_attention(GP * g - 2)
                for h, name in enumerate(KEYS):
                    if unit_owner(name)[1]:
                        dve.wait_ge(unit, gr.done(name))
                        dve.tensor_copy(kf[:, h, :], ring[gr.bank(name)][:, :]).then_inc(dve_ev, 1)
                    if first and h in (3, 7, 11):
                        split_w1(h // 4)
                    if not last and h == 11:
                        prep_stats(g + 1)
                    if not first:
                        if h == 3 and not (isinstance(g, int) and g == 1):
                            route_b(g - 2)
                        if h == 7:
                            add_attention(GP * g - 1)
                            dve.wait_ge(att_ok, GP * g)
                            norm_stats(lambda t: xs[:, r * GP + t, :], norm[1], s1_ok, r)
                        if h == 15:
                            dve.wait_ge(xp_ok, GP * r + GP)
                            norm_stats(lambda t: xp[:, t, :], norm[2], s2_ok, r)
                for i in range(GP):
                    n, par = GP * g + i, i % 2
                    if not (first and i < 2):
                        dve.wait_ge(t_full, 2 * n - 2)
                    shift_half(n, par, 0)
                    shift_half(n, par, 1)
                    if i == 0:
                        dve.wait_ge(bo_ok, g + 1)
                    normalize_half(n, par, 0)
                    normalize_half(n, par, 1)
                    if 0 < i < 3:
                        add_attention(n - 1)
                    if i == 1 and not first:
                        route_a(r, ring[gr.bank("RL")], gr.done("RL"), gr.done("RL", 1),
                                first=isinstance(g, int) and g == 1)
                    if i == 2 and not first:
                        route_c(r, ring[gr.bank("RX")], gr.done("RX"))
                if not last:
                    prep_units(gr)

            prep_units(start)
            dve.wait_ge(fold_ps, 1)
            dve.tensor_tensor(rb_sum[:, :], bank[6][:, 0:E], rb_b[:, :], ALU.add).then_inc(fold_ok, 1)
            dve.tensor_scalar(rW_g[:, :], rW_s[:, :], gc, None, ALU.mult).then_inc(w1_ok, 1)
            dve.tensor_copy(next_slot[:, :], region[:, :]).then_inc(w1_ok, 1)
            group(0, first=True)
            group(1)
            with dve.Fori(2, NG - 1) as g:
                group(g)
            group(NG - 1, last=True)
            add_attention(NP - 2)
            add_attention(NP - 1)
            dve.wait_ge(att_ok, NP)
            norm_stats(lambda t: xs[:, (NG - 1) * GP + t, :], norm[1], s1_ok, NG - 1)
            route_b(NG - 2)
            dve.wait_ge(xp_ok, GP * NG)
            norm_stats(lambda t: xp[:, t, :], norm[2], s2_ok, NG - 1)
            route_a(NG - 1, ring[2], TAIL_UNIT + 3, TAIL_DVE + 1, zlast, first=True)
            route_c(NG - 1, ring[3], TAIL_UNIT + 4, slot_ix_last)

            count = [0]

            def step(ins):
                count[0] += 1
                ins.then_inc(tab, 1)
                dve.wait_ge(tab, count[0])

            dve.wait_ge(dve_ev, TAIL_DVE + 2)
            step(dve.tensor_copy(next_i[:, :], next_slot[:, :]))
            assert count[0] == TAB_NEXT
            step(dve.tensor_tensor(n_tok, next_slot[:, :], region[:, :], ALU.subtract))
            step(dve.tensor_tensor(reg_cmp, n_tok.unsqueeze(2).to_broadcast([P, E, NB_MAX]),
                                   k_tile[:, :].unsqueeze(1).to_broadcast([P, E, NB_MAX]), ALU.is_gt))
            step(dve.reduce_sum(n_tile, reg_cmp, AX_X))
            step(dve.tensor_tensor(tri, rank[:, :].unsqueeze(1).to_broadcast([P, E, E]),
                                   rank[:, :].unsqueeze(2).to_broadcast([P, E, E]), ALU.is_ge))
            step(dve.tensor_tensor(tri_n, tri, n_tile.unsqueeze(1).to_broadcast([P, E, E]), ALU.mult))
            step(dve.reduce_sum(tile_end, tri_n, AX_X))
            dve.wait_ge(tn_ok, 1)
            step(dve.tensor_tensor(tile_cmp, tile_no.unsqueeze(2).to_broadcast([P, NT, E]),
                                   tile_end.unsqueeze(1).to_broadcast([P, NT, E]), ALU.is_ge))
            step(dve.reduce_sum(tile_e, tile_cmp, AX_X))
            step(dve.tensor_tensor(tile_cnt, tile_cmp, n_tile.unsqueeze(1).to_broadcast([P, NT, E]), ALU.mult))
            step(dve.reduce_sum(tile_st, tile_cnt, AX_X))
            step(dve.tensor_scalar(tile_live, tile_e, float(E), float(TILE), ALU.is_lt, ALU.mult))
            step(dve.tensor_tensor(tile_st, tile_no, tile_st, ALU.subtract))
            step(dve.tensor_tensor(tile_st, tile_st, tile_live, ALU.mult))
            step(dve.scalar_tensor_tensor(out=tile_row, in0=tile_e, scalar=float(REGION), in1=tile_st,
                                          op0=ALU.mult, op1=ALU.add))
            step(dve.tensor_copy(tile_row_i[:, :], tile_row))
            step(dve.tensor_scalar(tile_code, tile_e, -1.0, float(E), ALU.mult, ALU.add))
            step(dve.tensor_scalar(tile_st, tile_e, float(E - 1), None, ALU.min))
            step(dve.tensor_copy(tile_e_i[:, :], tile_st))
            assert count[0] == TAB_ALL
            route_b(NG - 1)

            dve.wait_ge(fold_ps, 2)
            dve.tensor_tensor(experts[:, :, 2 * HF + B1:2 * HF + B2],
                              bank[6][:, 0:E * FC].rearrange("p (e c) -> p e c", c=FC),
                              b1c.rearrange("p (e c) -> p e c", c=FC), ALU.add).then_inc(w1_ok, 1)
            dve.wait_ge(w1_ok, 6)

            def weights(s, deep):
                e = dve.value_load(tile_e_i[0:1, bass.ds(s, 1)], min_val=0, max_val=E - 1)
                src = experts[:, bass.ds(e, 1), :].rearrange("p a c -> p (a c)")
                if not isinstance(s, int) or s >= DEEP:
                    dve.wait_ge(dn_ps, s - DEEP + 1)
                dve.tensor_copy(w_r[deep], src[:, 0:2 * HF]).then_inc(wc_ok, 1)
                dve.tensor_copy(w_f[deep], src[:, 2 * HF:]).then_inc(wc_ok, 1)

            def lo_part(s, deep):
                dve.wait_ge(ch_hi, s + 1)
                if not isinstance(s, int) or s >= DEEP:
                    dve.wait_ge(up_ps, s - DEEP + 1)
                dve.tensor_tensor(z_lo[deep], bank[deep % 2][:, 0:TILE], z_hi[deep].bitcast(F32),
                                  ALU.subtract).then_inc(cl_lo, 1)

            def destinations(s, deep):
                dve.wait_ge(zi[deep], 4 * (s - deep) + 16)
                dve.tensor_scalar(ix_f[deep][:, 0, :], zin[deep][:, :, D + 1], tile_code[:, bass.ds(s, 1)],
                                  float(-NTOK), ALU.is_equal, ALU.mult).then_inc(yi_st, 1)
                dve.wait_ge(yi_st, 2 * s + 1)
                dve.scalar_tensor_tensor(out=ix_f[deep][:, 1, :], in0=ix_f[deep][:, 0, :], scalar=float(NTOK),
                                         in1=zin[deep][:, :, D], op0=ALU.add, op1=ALU.add).then_inc(yi_st, 1)

            def places(s, deep):
                dve.wait_ge(yi_st, 2 * s + 2)
                if not isinstance(s, int) or s >= DEEP:
                    dve.wait_ge(out_s[deep], 4 * TJ * (s - deep))
                dve.tensor_tensor(ix_i[deep][:, :], ix_f[deep][:, 1, :], pad_ix[:, deep, :], ALU.min).then_inc(yi_ok, 1)

            def tile_in(s, deep):
                weights(s, deep)
                destinations(s, deep)
                lo_part(s, deep)

            for s in range(2 * DEEP):
                tile_in(s, s % DEEP)
                if s >= 3:
                    places(s - 3, (s - 3) % DEEP)
            with dve.Fori(1, NT // (2 * DEEP)) as ss:
                for k in range(2 * DEEP):
                    tile_in(2 * DEEP * ss + k, k % DEEP)
                    places(2 * DEEP * ss + k - 3, (k - 3) % DEEP)
            for s in range(NT - 3, NT):
                places(s, s % DEEP)

            def add_experts(g, buf):
                dve.wait_ge(yl[buf], 8 * (g - buf) + 32)
                for k in range(2):
                    if k == 1:
                        dve.wait_ge(fin, 2 * GP * g + GP)
                    for t in range(GP):
                        dve.scalar_tensor_tensor(
                            out=xs[:, g * GP + t, :], in0=y_in[buf][:, k, t, :],
                            scalar=wgt[:, k, bass.ds(g * GP + t, 1)], in1=xs[:, g * GP + t, :],
                            op0=ALU.mult, op1=ALU.add).then_inc(fin, 1)

            dve.wait_ge(base_ok, NG)
            with dve.Fori(0, NG // 4) as gg:
                for buf in range(4):
                    add_experts(4 * gg + buf, buf)


_INS = ['x', 'ctx_1024', 'mask_BxS2_bf0', 'L0_xattn_Wq', 'L0_xattn_Wk', 'L0_xattn_Wv', 'L0_xattn_Wo', 'L0_xattn_bo',
        'L0_ffn_ln_g', 'L0_ffn_ln_b', 'L0_ffn_rW', 'L0_ffn_rb', 'L0_ffn_W1', 'L0_ffn_b1', 'L0_ffn_W2', 'L0_ffn_b2']
_OUTS = [((128, 64, 128), 'float32')]


def kernel(**inputs):
    import numpy as _np
    import concourse.bacc as _bacc
    from concourse import mybir as _mybir
    from concourse.bass_utils import run_bass_kernel_spmd as _run

    nc = _bacc.Bacc("TRN2", target_bir_lowering=False, num_devices=1)
    arrays, args = {}, []
    for name in _INS:
        a = _np.ascontiguousarray(inputs[name])
        arrays[f"in_{name}_dram"] = a
        args.append(nc.dram_tensor(f"in_{name}_dram", a.shape, _mybir.dt.from_np(a.dtype), kind="ExternalInput").ap())
    for i, (shape, dtype) in enumerate(_OUTS):
        dt = _mybir.dt.from_np(_np.dtype(dtype))
        args.append(nc.dram_tensor(f"out_{i}_dram", shape, dt, kind="ExternalOutput").ap())
    xattn_ffn_kernel(nc, *args)
    r = _run(nc, [arrays], core_ids=[0])
    got = tuple(r.results[0][f"out_{i}_dram"] for i in range(len(_OUTS)))
    return got[0]
```
